# Optimizing a Trainium2 kernel written in Bass

```python
import numpy as np
import jax
import jax.numpy as jnp

def _softmax(x, axis=-1):
    return jax.nn.softmax(x, axis=axis)

def _gelu(x):
    return jax.nn.gelu(x, approximate=True)

def _silu(x):
    return jax.nn.silu(x)

def _sigmoid(x):
    return jax.nn.sigmoid(x)

def _layernorm(x, axis=-1, eps=1e-05):
    m = jnp.mean(x, axis=axis, keepdims=True)
    v = jnp.var(x, axis=axis, keepdims=True)
    return (x - m) / jnp.sqrt(v + eps)

def _scatter_add(tgt, idx, src, axis=0):
    return tgt.at[idx].add(src)

def _segment_sum(src, seg, n):
    return jax.ops.segment_sum(src, seg, n)
kernel_name = 'mk_decoder_postln_d2_seqx_r4_061b62'

def setup_inputs(seed: int=0):
    np.random.seed(seed)
    _w = jnp.asarray

    def _rec_inputs():
        import jax
        import jax.numpy as jnp
        _rk = jax.random.key(seed)
        x = -0.0002928 + 1 * jax.random.normal(jax.random.fold_in(_rk, 1), (8, 256, 256), jnp.float32)
        _lenS = 256 - jax.random.randint(jax.random.fold_in(_rk, 7), (8,), 0, max(1, 256 // 4) + 1, jnp.int32)
        _lenS2 = 256 - jax.random.randint(jax.random.fold_in(_rk, 8), (8,), 0, max(1, 256 // 4) + 1, jnp.int32)
        _ctx_1024P = jax.random.normal(jax.random.fold_in(_rk, 11), (8, 16, 256), jnp.float32)
        _ctx_1024c = jax.random.dirichlet(jax.random.fold_in(_rk, 511), 0.3 * jnp.ones((16,), jnp.float32), (8, 256))
        _ctx_1024t = jnp.einsum('bsk,bkd->bsd', _ctx_1024c, _ctx_1024P)
        _ctx_1024t = _ctx_1024t * jax.lax.rsqrt(jnp.mean(jnp.square(_ctx_1024t)) + 1e-12) * 0.953939
        ctx_1024 = -1.39393e-06 + 0.999914 * (_ctx_1024t + 0.3 * jax.random.normal(jax.random.fold_in(_rk, 611), (8, 256, 256), jnp.float32))
        return (x, ctx_1024)
    x, ctx_1024 = _rec_inputs()

    def _L0_attn_setup():
        import jax, jax.numpy as jnp
        import numpy as np
        D_MODEL = 256
        NHEAD = 16
        HID = int(D_MODEL * 4.0 * (2.0 / 3.0))
        EPS = 1e-05

        def _ln(x, w, b):
            m = jnp.mean(x, axis=-1, keepdims=True)
            v = jnp.mean((x - m) ** 2, axis=-1, keepdims=True)
            return (x - m) / jnp.sqrt(v + EPS) * w + b
        key = jax.random.key(seed)
        ks = jax.random.split(key, 10)
        w = lambda k, shape: jax.random.normal(k, shape, jnp.float32) * 0.02
        D = D_MODEL
        inp = {'x': jax.random.normal(ks[0], (1, 512, D), jnp.float32), 'norm1_w': jnp.ones((D,), jnp.float32), 'norm1_b': jnp.zeros((D,), jnp.float32), 'wq': w(ks[1], (D, D)), 'bq': jnp.zeros((D,), jnp.float32), 'wk': w(ks[2], (D, D)), 'bk': jnp.zeros((D,), jnp.float32), 'wv': w(ks[3], (D, D)), 'bv': jnp.zeros((D,), jnp.float32), 'wg': w(ks[4], (D, D)), 'bg': jnp.zeros((D,), jnp.float32), 'wo': w(ks[5], (D, D)), 'bo': jnp.zeros((D,), jnp.float32), 'gn_w': jnp.ones((D,), jnp.float32), 'gn_b': jnp.zeros((D,), jnp.float32), 'norm2_w': jnp.ones((D,), jnp.float32), 'norm2_b': jnp.zeros((D,), jnp.float32), 'w_in': w(ks[6], (D, 2 * HID)), 'b_in': jnp.zeros((2 * HID,), jnp.float32), 'w_out': w(ks[7], (HID, D)), 'b_out': jnp.zeros((D,), jnp.float32)}
        return inp
    _L0_attn_all = _L0_attn_setup()
    _L0_attn_in = {k: v for k, v in _L0_attn_all.items() if k in ('norm1_w', 'norm1_b', 'wq', 'bq', 'wk', 'bk', 'wv', 'bv', 'wg', 'bg', 'wo', 'bo', 'gn_w', 'gn_b', 'norm2_w', 'norm2_b', 'w_in', 'b_in', 'w_out', 'b_out')}
    del _L0_attn_all

    def _L0_xattn_setup():
        import jax, jax.numpy as jnp
        import numpy as np
        D_MODEL = 256
        NUM_HEADS = 16
        D_K = D_MODEL // NUM_HEADS
        key = jax.random.key(seed)
        ks = jax.random.split(key, 11)
        B, S = (2, 512)
        s = 1.0 / np.sqrt(D_MODEL)
        return {'q': jax.random.normal(ks[0], (B, S, D_MODEL), jnp.float32), 'k': jax.random.normal(ks[1], (B, S, D_MODEL), jnp.float32), 'v': jax.random.normal(ks[2], (B, S, D_MODEL), jnp.float32), 'w_q': jax.random.normal(ks[3], (D_MODEL, D_MODEL), jnp.float32) * s, 'b_q': jnp.zeros((D_MODEL,), jnp.float32), 'w_k': jax.random.normal(ks[4], (D_MODEL, D_MODEL), jnp.float32) * s, 'b_k': jnp.zeros((D_MODEL,), jnp.float32), 'w_v': jax.random.normal(ks[5], (D_MODEL, D_MODEL), jnp.float32) * s, 'b_v': jnp.zeros((D_MODEL,), jnp.float32), 'w_o': jax.random.normal(ks[6], (D_MODEL, D_MODEL), jnp.float32) * s, 'b_o': jnp.zeros((D_MODEL,), jnp.float32)}
    _L0_xattn_all = _L0_xattn_setup()
    _L0_xattn_in = {k: v for k, v in _L0_xattn_all.items() if k in ('w_q', 'b_q', 'w_k', 'b_k', 'w_v', 'b_v', 'w_o', 'b_o')}
    del _L0_xattn_all

    def _L0_ffn_setup():
        import jax, jax.numpy as jnp
        import numpy as np
        DIM = 256

        def _reference_tuple_inner(x, W_r, W_k, W_v, mu_r, mu_k):
            B, T, C = x.shape
            x_prev = jnp.concatenate([jnp.zeros((B, 1, C), x.dtype), x[:, :-1, :]], axis=1)
            xr = mu_r * x + (1.0 - mu_r) * x_prev
            xk = mu_k * x + (1.0 - mu_k) * x_prev
            r = jax.nn.sigmoid(jnp.einsum('btc,dc->btd', xr, W_r))
            k = jnp.einsum('btc,dc->btd', xk, W_k)
            k_act = jnp.square(jax.nn.relu(k))
            out = r * jnp.einsum('btc,dc->btd', k_act, W_v)
            new_state = x[:, -1, :]
            return (out, new_state)
        key = jax.random.key(seed)
        ks = jax.random.split(key, 6)
        B, T, C = (8, 512, DIM)
        x = jax.random.normal(ks[0], (B, T, C), dtype=jnp.float32)
        s = 1.0 / np.sqrt(C)
        W_r = jax.random.uniform(ks[1], (C, C), jnp.float32, -s, s)
        W_k = jax.random.uniform(ks[2], (C, C), jnp.float32, -s, s)
        W_v = jax.random.uniform(ks[3], (C, C), jnp.float32, -s, s)
        mu_r = jax.random.uniform(ks[4], (C,), jnp.float32)
        mu_k = jax.random.uniform(ks[5], (C,), jnp.float32)
        return {'x': x, 'W_r': W_r, 'W_k': W_k, 'W_v': W_v, 'mu_r': mu_r, 'mu_k': mu_k}
    _L0_ffn_all = _L0_ffn_setup()
    _L0_ffn_in = {k: v for k, v in _L0_ffn_all.items() if k in ('W_r', 'W_k', 'W_v', 'mu_r', 'mu_k')}
    del _L0_ffn_all

    def _L1_attn_setup():
        import jax, jax.numpy as jnp
        import numpy as np
        B, S, D, H, R = (2, 512, 256, 16, 64)
        HD = D // H
        VOCAB = 2 * R + 1
        key = jax.random.key(seed)
        ks = jax.random.split(key, 7)
        s = 0.02
        return {'x': jax.random.normal(ks[0], (B, S, D), jnp.float32), 'W_qkv': jax.random.normal(ks[1], (D, 3 * D), jnp.float32) * s, 'b_qkv': jnp.zeros((3 * D,), jnp.float32), 'W_out': jax.random.normal(ks[2], (D, D), jnp.float32) * s, 'b_out': jnp.zeros((D,), jnp.float32), 'rel_emb_k': jax.random.normal(ks[3], (VOCAB, HD), jnp.float32) * s, 'rel_emb_v': jax.random.normal(ks[4], (VOCAB, HD), jnp.float32) * s}
    _L1_attn_all = _L1_attn_setup()
    _L1_attn_in = {k: v for k, v in _L1_attn_all.items() if k in ('W_qkv', 'b_qkv', 'W_out', 'b_out', 'rel_emb_k', 'rel_emb_v')}
    del _L1_attn_all

    def _L1_xattn_setup():
        import jax, jax.numpy as jnp
        import numpy as np
        import math
        EPS = 1e-08
        LN_EPS = 1e-05
        B, S, E, NH = (2, 512, 256, 4)
        DH = E // NH

        def _mlstm_cell(q, k, v, igate_w, igate_b, fgate_w, fgate_b, out_w):
            Bq, Sq, Eq = q.shape
            if_in = jnp.concatenate([q, k, v], axis=-1)
            ig = jnp.einsum('bsf,hf->bsh', if_in, igate_w) + igate_b
            fg = jnp.einsum('bsf,hf->bsh', if_in, fgate_w) + fgate_b
            ig = jnp.transpose(ig, (0, 2, 1))[..., None]
            fg = jnp.transpose(fg, (0, 2, 1))[..., None]
            qh = q.reshape(Bq, Sq, NH, DH).transpose(0, 2, 1, 3)
            kh = k.reshape(Bq, Sq, NH, DH).transpose(0, 2, 1, 3)
            vh = v.reshape(Bq, Sq, NH, DH).transpose(0, 2, 1, 3)
            log_fg = jax.nn.log_sigmoid(fg)
            cs = jnp.cumsum(log_fg, axis=2)
            cs_shift = jnp.concatenate([jnp.zeros_like(cs[:, :, :1]), cs[:, :, :-1]], axis=2)
            logfg_mat = cs - jnp.swapaxes(cs_shift, -2, -1)
            ltr = jnp.tril(jnp.ones((Sq, Sq), dtype=bool))
            logfg_mat = jnp.where(ltr, logfg_mat, -jnp.inf)
            log_D = logfg_mat + jnp.swapaxes(ig, -2, -1)
            max_log_D = jnp.max(log_D, axis=-1, keepdims=True)
            D = jnp.exp(log_D - max_log_D)
            qk = jnp.einsum('bhsd,bhtd->bhst', qh, kh / math.sqrt(DH))
            C = qk * D
            sum_C_abs = jnp.abs(jnp.sum(C, axis=-1, keepdims=True))
            normaliser = jnp.maximum(sum_C_abs, jnp.exp(-max_log_D))
            C_norm = C / (normaliser + EPS)
            h = jnp.einsum('bhst,bhtd->bhsd', C_norm, vh)
            mean = jnp.mean(h, axis=-1, keepdims=True)
            var = jnp.mean((h - mean) ** 2, axis=-1, keepdims=True)
            h_norm = (h - mean) / jnp.sqrt(var + LN_EPS)
            scale = (1.0 + out_w).reshape(1, NH, 1, DH)
            h_norm = h_norm * scale
            return h_norm.transpose(0, 2, 1, 3).reshape(Bq, Sq, Eq)
        key = jax.random.key(seed)
        ks = jax.random.split(key, 7)
        std_g = math.sqrt(2.0 / (5.0 * 3 * E))
        return {'q': jax.random.normal(ks[0], (B, S, E), dtype=jnp.float32), 'k': jax.random.normal(ks[1], (B, S, E), dtype=jnp.float32), 'v': jax.random.normal(ks[2], (B, S, E), dtype=jnp.float32), 'igate_w': jax.random.normal(ks[3], (NH, 3 * E), dtype=jnp.float32) * std_g, 'igate_b': jax.random.normal(ks[4], (NH,), dtype=jnp.float32) * 0.1, 'fgate_w': jax.random.normal(ks[5], (NH, 3 * E), dtype=jnp.float32) * std_g, 'fgate_b': jnp.linspace(3.4, 6.0, NH, dtype=jnp.float32), 'out_w': jnp.zeros((E,), dtype=jnp.float32)}
    _L1_xattn_all = _L1_xattn_setup()
    _L1_xattn_in = {k: v for k, v in _L1_xattn_all.items() if k in ('igate_w', 'igate_b', 'fgate_w', 'fgate_b', 'out_w')}
    del _L1_xattn_all

    def _L1_ffn_setup():
        import jax, jax.numpy as jnp
        import numpy as np
        H = 8
        KD = 128
        TOPK = 8
        NUM_KEYS = 64
        N_EXPERTS = NUM_KEYS * NUM_KEYS
        N_DIM = 256
        BN_EPS = 1e-05

        def gelu_new(x):
            c = jnp.sqrt(jnp.asarray(2.0 / jnp.pi, x.dtype))
            return 0.5 * x * (1.0 + jnp.tanh(c * (x + 0.044715 * x * x * x)))
        key = jax.random.key(seed)
        ks = jax.random.split(key, 5)
        b, s = (2, 256)
        x = jax.random.normal(ks[0], (b, s, N_DIM), dtype=jnp.float32)
        w_q = jax.random.normal(ks[1], (N_DIM, 2 * H * KD), dtype=jnp.float32) * 0.02
        bn_gamma = jnp.ones((2 * H * KD,), dtype=jnp.float32)
        bn_beta = jnp.zeros((2 * H * KD,), dtype=jnp.float32)
        keys = jax.random.normal(ks[2], (H, NUM_KEYS, 2, KD), dtype=jnp.float32) * 0.02
        down_embed = jax.random.normal(ks[3], (N_EXPERTS, N_DIM), dtype=jnp.float32) * 0.02
        up_embed = jax.random.normal(ks[4], (N_EXPERTS, N_DIM), dtype=jnp.float32) * 0.02
        return {'x': x, 'w_q': w_q, 'bn_gamma': bn_gamma, 'bn_beta': bn_beta, 'keys': keys, 'down_embed': down_embed, 'up_embed': up_embed}
    _L1_ffn_all = _L1_ffn_setup()
    _L1_ffn_in = {k: v for k, v in _L1_ffn_all.items() if k in ('w_q', 'bn_gamma', 'bn_beta', 'keys', 'down_embed', 'up_embed')}
    del _L1_ffn_all
    return {'x': x, 'ctx_1024': ctx_1024, 'L0_attn_norm1_w': _L0_attn_in['norm1_w'], 'L0_attn_norm1_b': _L0_attn_in['norm1_b'], 'L0_attn_wq': _L0_attn_in['wq'], 'L0_attn_bq': _L0_attn_in['bq'], 'L0_attn_wk': _L0_attn_in['wk'], 'L0_attn_bk': _L0_attn_in['bk'], 'L0_attn_wv': _L0_attn_in['wv'], 'L0_attn_bv': _L0_attn_in['bv'], 'L0_attn_wg': _L0_attn_in['wg'], 'L0_attn_bg': _L0_attn_in['bg'], 'L0_attn_wo': _L0_attn_in['wo'], 'L0_attn_bo': _L0_attn_in['bo'], 'L0_attn_gn_w': _L0_attn_in['gn_w'], 'L0_attn_gn_b': _L0_attn_in['gn_b'], 'L0_attn_norm2_w': _L0_attn_in['norm2_w'], 'L0_attn_norm2_b': _L0_attn_in['norm2_b'], 'L0_attn_w_in': _L0_attn_in['w_in'], 'L0_attn_b_in': _L0_attn_in['b_in'], 'L0_attn_w_out': _L0_attn_in['w_out'], 'L0_attn_b_out': _L0_attn_in['b_out'], 'L0_xattn_w_q': _L0_xattn_in['w_q'], 'L0_xattn_b_q': _L0_xattn_in['b_q'], 'L0_xattn_w_k': _L0_xattn_in['w_k'], 'L0_xattn_b_k': _L0_xattn_in['b_k'], 'L0_xattn_w_v': _L0_xattn_in['w_v'], 'L0_xattn_b_v': _L0_xattn_in['b_v'], 'L0_xattn_w_o': _L0_xattn_in['w_o'], 'L0_xattn_b_o': _L0_xattn_in['b_o'], 'L0_ffn_W_r': _L0_ffn_in['W_r'], 'L0_ffn_W_k': _L0_ffn_in['W_k'], 'L0_ffn_W_v': _L0_ffn_in['W_v'], 'L0_ffn_mu_r': _L0_ffn_in['mu_r'], 'L0_ffn_mu_k': _L0_ffn_in['mu_k'], 'L1_attn_W_qkv': _L1_attn_in['W_qkv'], 'L1_attn_b_qkv': _L1_attn_in['b_qkv'], 'L1_attn_W_out': _L1_attn_in['W_out'], 'L1_attn_b_out': _L1_attn_in['b_out'], 'L1_attn_rel_emb_k': _L1_attn_in['rel_emb_k'], 'L1_attn_rel_emb_v': _L1_attn_in['rel_emb_v'], 'L1_xattn_igate_w': _L1_xattn_in['igate_w'], 'L1_xattn_igate_b': _L1_xattn_in['igate_b'], 'L1_xattn_fgate_w': _L1_xattn_in['fgate_w'], 'L1_xattn_fgate_b': _L1_xattn_in['fgate_b'], 'L1_xattn_out_w': _L1_xattn_in['out_w'], 'L1_ffn_w_q': _L1_ffn_in['w_q'], 'L1_ffn_bn_gamma': _L1_ffn_in['bn_gamma'], 'L1_ffn_bn_beta': _L1_ffn_in['bn_beta'], 'L1_ffn_keys': _L1_ffn_in['keys'], 'L1_ffn_down_embed': _L1_ffn_in['down_embed'], 'L1_ffn_up_embed': _L1_ffn_in['up_embed']}

def reference(x, ctx_1024, L0_attn_norm1_w, L0_attn_norm1_b, L0_attn_wq, L0_attn_bq, L0_attn_wk, L0_attn_bk, L0_attn_wv, L0_attn_bv, L0_attn_wg, L0_attn_bg, L0_attn_wo, L0_attn_bo, L0_attn_gn_w, L0_attn_gn_b, L0_attn_norm2_w, L0_attn_norm2_b, L0_attn_w_in, L0_attn_b_in, L0_attn_w_out, L0_attn_b_out, L0_xattn_w_q, L0_xattn_b_q, L0_xattn_w_k, L0_xattn_b_k, L0_xattn_w_v, L0_xattn_b_v, L0_xattn_w_o, L0_xattn_b_o, L0_ffn_W_r, L0_ffn_W_k, L0_ffn_W_v, L0_ffn_mu_r, L0_ffn_mu_k, L1_attn_W_qkv, L1_attn_b_qkv, L1_attn_W_out, L1_attn_b_out, L1_attn_rel_emb_k, L1_attn_rel_emb_v, L1_xattn_igate_w, L1_xattn_igate_b, L1_xattn_fgate_w, L1_xattn_fgate_b, L1_xattn_out_w, L1_ffn_w_q, L1_ffn_bn_gamma, L1_ffn_bn_beta, L1_ffn_keys, L1_ffn_down_embed, L1_ffn_up_embed):
    import jax
    import jax.numpy as jnp

    def _L0_attn_ref(x, norm1_w, norm1_b, wq, bq, wk, bk, wv, bv, wg, bg, wo, bo, gn_w, gn_b, norm2_w, norm2_b, w_in, b_in, w_out, b_out):
        import jax, jax.numpy as jnp
        import numpy as np
        D_MODEL = 256
        NHEAD = 16
        HID = int(D_MODEL * 4.0 * (2.0 / 3.0))
        EPS = 1e-05

        def _ln(x, w, b):
            m = jnp.mean(x, axis=-1, keepdims=True)
            v = jnp.mean((x - m) ** 2, axis=-1, keepdims=True)
            return (x - m) / jnp.sqrt(v + EPS) * w + b
        B, S, D = x.shape
        H = NHEAD
        hd = D // H
        xn = _ln(x, norm1_w, norm1_b)
        q = (xn @ wq + bq).reshape(B, S, H, hd).transpose(0, 2, 1, 3)
        k = (xn @ wk + bk).reshape(B, S, H, hd).transpose(0, 2, 1, 3)
        v = (xn @ wv + bv).reshape(B, S, H, hd).transpose(0, 2, 1, 3)
        gamma = 1.0 - jnp.exp2(-5.0 - jnp.arange(H, dtype=jnp.float32))
        n = jnp.arange(S)
        diff = (n[:, None] - n[None, :]).astype(jnp.float32)
        Dmat = jnp.where(diff >= 0, jnp.exp(jnp.log(gamma)[:, None, None] * diff), 0.0)
        scores = jnp.einsum('bhnd,bhmd->bhnm', q, k) * hd ** (-0.5)
        ret = jnp.einsum('bhnm,bhmd->bhnd', scores * Dmat, v)
        ret = ret.transpose(0, 2, 1, 3)
        mu = jnp.mean(ret, axis=-1, keepdims=True)
        var = jnp.mean((ret - mu) ** 2, axis=-1, keepdims=True)
        gn = ((ret - mu) / jnp.sqrt(var + EPS)).reshape(B, S, D) * gn_w + gn_b
        gate = jax.nn.silu(xn @ wg + bg)
        h = gate * gn @ wo + bo
        x = x + h
        x2 = _ln(x, norm2_w, norm2_b)
        uv = x2 @ w_in + b_in
        u, g = jnp.split(uv, 2, axis=-1)
        x = x + (jax.nn.silu(u) * g @ w_out + b_out)
        return x

    def _L0_xattn_ref(q, k, v, w_q, b_q, w_k, b_k, w_v, b_v, w_o, b_o):
        import jax, jax.numpy as jnp
        import numpy as np
        D_MODEL = 256
        NUM_HEADS = 16
        D_K = D_MODEL // NUM_HEADS
        B, S, _ = q.shape
        H, Dk = (NUM_HEADS, D_K)

        def split_heads(x):
            return x.reshape(B, S, H, Dk).transpose(0, 2, 1, 3)
        qh = split_heads(q @ w_q.T + b_q)
        kh = split_heads(k @ w_k.T + b_k)
        vh = split_heads(v @ w_v.T + b_v)
        scale = 1.0 / jnp.sqrt(jnp.asarray(Dk, qh.dtype))
        scores = jnp.einsum('bhsd,bhtd->bhst', qh, kh) * scale
        attn = jax.nn.softmax(scores, axis=-1)
        out = jnp.einsum('bhst,bhtd->bhsd', attn, vh)
        out = out.transpose(0, 2, 1, 3).reshape(B, S, H * Dk)
        return out @ w_o.T + b_o

    def _L0_ffn_ref(x, W_r, W_k, W_v, mu_r, mu_k):
        import jax, jax.numpy as jnp
        import numpy as np
        DIM = 256

        def _reference_tuple_inner(x, W_r, W_k, W_v, mu_r, mu_k):
            B, T, C = x.shape
            x_prev = jnp.concatenate([jnp.zeros((B, 1, C), x.dtype), x[:, :-1, :]], axis=1)
            xr = mu_r * x + (1.0 - mu_r) * x_prev
            xk = mu_k * x + (1.0 - mu_k) * x_prev
            r = jax.nn.sigmoid(jnp.einsum('btc,dc->btd', xr, W_r))
            k = jnp.einsum('btc,dc->btd', xk, W_k)
            k_act = jnp.square(jax.nn.relu(k))
            out = r * jnp.einsum('btc,dc->btd', k_act, W_v)
            new_state = x[:, -1, :]
            return (out, new_state)
        return _reference_tuple_inner(x, W_r, W_k, W_v, mu_r, mu_k)[0]

    def _L1_attn_ref(x, W_qkv, b_qkv, W_out, b_out, rel_emb_k, rel_emb_v):
        import jax, jax.numpy as jnp
        import numpy as np
        B, S, D, H, R = (2, 512, 256, 16, 64)
        HD = D // H
        VOCAB = 2 * R + 1
        b, s, d = x.shape
        hd = d // H
        idx = jnp.arange(s)
        dist = jnp.clip(idx[None, :] - idx[:, None], -R, R) + R
        pe_k = rel_emb_k[dist]
        pe_v = rel_emb_v[dist]
        qkv = (x @ W_qkv + b_qkv).reshape(b, s, 3, H, hd)
        qkv = jnp.transpose(qkv, (2, 0, 3, 1, 4))
        q, k, v = (qkv[0], qkv[1], qkv[2])
        q = q / jnp.sqrt(jnp.asarray(hd, x.dtype))
        score = jnp.einsum('bhqd,bhkd->bhqk', q, k) + jnp.einsum('bhqd,qkd->bhqk', q, pe_k)
        attn = jax.nn.softmax(score, axis=-1)
        ctx = jnp.einsum('bhqk,bhkd->bhqd', attn, v) + jnp.einsum('bhqk,qkd->bhqd', attn, pe_v)
        ctx = jnp.transpose(ctx, (0, 2, 1, 3)).reshape(b, s, d)
        return ctx @ W_out + b_out

    def _L1_xattn_ref(q, k, v, igate_w, igate_b, fgate_w, fgate_b, out_w):
        import jax, jax.numpy as jnp
        import numpy as np
        import math
        EPS = 1e-08
        LN_EPS = 1e-05
        B, S, E, NH = (2, 512, 256, 4)
        DH = E // NH

        def _mlstm_cell(q, k, v, igate_w, igate_b, fgate_w, fgate_b, out_w):
            Bq, Sq, Eq = q.shape
            if_in = jnp.concatenate([q, k, v], axis=-1)
            ig = jnp.einsum('bsf,hf->bsh', if_in, igate_w) + igate_b
            fg = jnp.einsum('bsf,hf->bsh', if_in, fgate_w) + fgate_b
            ig = jnp.transpose(ig, (0, 2, 1))[..., None]
            fg = jnp.transpose(fg, (0, 2, 1))[..., None]
            qh = q.reshape(Bq, Sq, NH, DH).transpose(0, 2, 1, 3)
            kh = k.reshape(Bq, Sq, NH, DH).transpose(0, 2, 1, 3)
            vh = v.reshape(Bq, Sq, NH, DH).transpose(0, 2, 1, 3)
            log_fg = jax.nn.log_sigmoid(fg)
            cs = jnp.cumsum(log_fg, axis=2)
            cs_shift = jnp.concatenate([jnp.zeros_like(cs[:, :, :1]), cs[:, :, :-1]], axis=2)
            logfg_mat = cs - jnp.swapaxes(cs_shift, -2, -1)
            ltr = jnp.tril(jnp.ones((Sq, Sq), dtype=bool))
            logfg_mat = jnp.where(ltr, logfg_mat, -jnp.inf)
            log_D = logfg_mat + jnp.swapaxes(ig, -2, -1)
            max_log_D = jnp.max(log_D, axis=-1, keepdims=True)
            D = jnp.exp(log_D - max_log_D)
            qk = jnp.einsum('bhsd,bhtd->bhst', qh, kh / math.sqrt(DH))
            C = qk * D
            sum_C_abs = jnp.abs(jnp.sum(C, axis=-1, keepdims=True))
            normaliser = jnp.maximum(sum_C_abs, jnp.exp(-max_log_D))
            C_norm = C / (normaliser + EPS)
            h = jnp.einsum('bhst,bhtd->bhsd', C_norm, vh)
            mean = jnp.mean(h, axis=-1, keepdims=True)
            var = jnp.mean((h - mean) ** 2, axis=-1, keepdims=True)
            h_norm = (h - mean) / jnp.sqrt(var + LN_EPS)
            scale = (1.0 + out_w).reshape(1, NH, 1, DH)
            h_norm = h_norm * scale
            return h_norm.transpose(0, 2, 1, 3).reshape(Bq, Sq, Eq)
        return _mlstm_cell(q, k, v, igate_w, igate_b, fgate_w, fgate_b, out_w)

    def _L1_ffn_ref(x, w_q, bn_gamma, bn_beta, keys, down_embed, up_embed):
        import jax, jax.numpy as jnp
        import numpy as np
        H = 8
        KD = 128
        TOPK = 8
        NUM_KEYS = 64
        N_EXPERTS = NUM_KEYS * NUM_KEYS
        N_DIM = 256
        BN_EPS = 1e-05

        def gelu_new(x):
            c = jnp.sqrt(jnp.asarray(2.0 / jnp.pi, x.dtype))
            return 0.5 * x * (1.0 + jnp.tanh(c * (x + 0.044715 * x * x * x)))
        b, n, d = x.shape
        q = jnp.einsum('bnd,de->bne', x, w_q)
        mean = jnp.mean(q, axis=(0, 1))
        var = jnp.var(q, axis=(0, 1))
        q = (q - mean) * jax.lax.rsqrt(var + BN_EPS) * bn_gamma + bn_beta
        q = q.reshape(b, n, 2, H, KD).transpose(2, 0, 1, 3, 4)
        sim = jnp.einsum('pbnhd,hkpd->pbnhk', q, keys)
        sx, ix = jax.lax.top_k(sim[0], TOPK)
        sy, iy = jax.lax.top_k(sim[1], TOPK)
        all_scores = (sx[..., :, None] + sy[..., None, :]).reshape(b, n, H, TOPK * TOPK)
        all_indices = (ix[..., :, None] * NUM_KEYS + iy[..., None, :]).reshape(b, n, H, TOPK * TOPK)
        scores, pk = jax.lax.top_k(all_scores, TOPK)
        indices = jnp.take_along_axis(all_indices, pk, axis=-1)
        wd = down_embed[indices]
        wu = up_embed[indices]
        h = jnp.einsum('bnd,bnhkd->bnhk', x, wd)
        h = gelu_new(h)
        h = jax.nn.softmax(scores, axis=-1) * h
        out = jnp.einsum('bnhk,bnhkd->bnd', h, wu)
        return out
    x = _layernorm(x + _L0_attn_ref(x, L0_attn_norm1_w, L0_attn_norm1_b, L0_attn_wq, L0_attn_bq, L0_attn_wk, L0_attn_bk, L0_attn_wv, L0_attn_bv, L0_attn_wg, L0_attn_bg, L0_attn_wo, L0_attn_bo, L0_attn_gn_w, L0_attn_gn_b, L0_attn_norm2_w, L0_attn_norm2_b, L0_attn_w_in, L0_attn_b_in, L0_attn_w_out, L0_attn_b_out), axis=-1)
    x = _layernorm(x + _L0_xattn_ref(x, ctx_1024, ctx_1024, L0_xattn_w_q, L0_xattn_b_q, L0_xattn_w_k, L0_xattn_b_k, L0_xattn_w_v, L0_xattn_b_v, L0_xattn_w_o, L0_xattn_b_o), axis=-1)
    x = _layernorm(x + _L0_ffn_ref(x, L0_ffn_W_r, L0_ffn_W_k, L0_ffn_W_v, L0_ffn_mu_r, L0_ffn_mu_k), axis=-1)
    x = _layernorm(x + _L1_attn_ref(x, L1_attn_W_qkv, L1_attn_b_qkv, L1_attn_W_out, L1_attn_b_out, L1_attn_rel_emb_k, L1_attn_rel_emb_v), axis=-1)
    x = _layernorm(x + _L1_xattn_ref(x, ctx_1024, ctx_1024, L1_xattn_igate_w, L1_xattn_igate_b, L1_xattn_fgate_w, L1_xattn_fgate_b, L1_xattn_out_w), axis=-1)
    x = _layernorm(x + _L1_ffn_ref(x, L1_ffn_w_q, L1_ffn_bn_gamma, L1_ffn_bn_beta, L1_ffn_keys, L1_ffn_down_embed, L1_ffn_up_embed), axis=-1)
    return x

_drawn_inputs = setup_inputs


def setup_inputs(seed=0):
    import zlib

    import numpy as np

    out = dict(_drawn_inputs(seed))
    spreads = {'L0_attn_norm1_w': (1.0, 0.6),
     'L0_attn_norm1_b': (0.0, 0.8),
     'L0_attn_bq': (0.0, 0.8),
     'L0_attn_bk': (0.0, 0.519),
     'L0_attn_bv': (0.0, 0.513),
     'L0_attn_bg': (0.0, 0.8),
     'L0_attn_bo': (0.0, 0.1),
     'L0_attn_gn_w': (1.0, 0.6),
     'L0_attn_gn_b': (0.0, 0.8),
     'L0_attn_norm2_w': (1.0, 0.6),
     'L0_attn_norm2_b': (0.0, 0.8),
     'L0_attn_b_in': (0.0, 0.8),
     'L0_attn_b_out': (0.0, 0.272),
     'L0_xattn_b_q': (0.0, 0.379),
     'L0_xattn_b_k': (0.0, 2.0),
     'L0_xattn_b_v': (0.0, 0.1),
     'L0_xattn_b_o': (0.0, 0.1),
     'L1_attn_b_qkv': (0.0, 0.1),
     'L1_attn_b_out': (0.0, 0.1),
     'L1_xattn_out_w': (0.0, 0.1),
     'L1_ffn_bn_gamma': (1.0, 0.6),
     'L1_ffn_bn_beta': (0.0, 0.8)}
    factors = {'L0_attn_w_in': 3.365,
     'L0_attn_w_out': 3.217,
     'L0_ffn_mu_r': 5.968,
     'L1_attn_rel_emb_k': 200.0,
     'L1_attn_rel_emb_v': 8.0,
     'L1_xattn_igate_b': 64.0,
     'L1_ffn_w_q': 8.0,
     'L1_ffn_keys': 8.0,
     'L1_ffn_down_embed': 8.0,
     'L1_ffn_up_embed': 8.0}
    for name, (base, spread) in spreads.items():
        noise = np.random.default_rng([zlib.crc32(name.encode()), seed]).standard_normal(out[name].shape)
        drawn = base * np.exp(spread * noise) if base else spread * noise
        out[name] = jnp.asarray(drawn.astype(out[name].dtype))
    for name, factor in factors.items():
        out[name] = (out[name] * factor).astype(out[name].dtype)
    return out
```

```python
from contextlib import ExitStack

import concourse.bass as bass
from concourse import mybir
import numpy as np

P = 128
BATCHES = 8
SEQ = 256
D = 256
DC = D // P
TT = SEQ // P
HEADS = 16
HD = D // HEADS
GROUPS = 4
HID = 682
HC = 6
LN_EPS = 1e-5

F32 = mybir.dt.float32
F16 = mybir.dt.float16
BF16 = mybir.dt.bfloat16
U32 = mybir.dt.uint32
U16 = mybir.dt.uint16
ALU = mybir.AluOpType
ACT = mybir.ActivationFunctionType
AX = mybir.AxisListType


def link(engine, instruction):
    engine.drain()
    return instruction


def over(ap, n):
    return ap.unsqueeze(ap.ndim).broadcast_to(list(ap.shape) + [n])


def batch_of(ap, n):
    return ap[bass.ds(n, 1)].rearrange("a (t p) d -> p (a t) d", p=P)


def load_all(engine, sem, pairs):
    for to, what in pairs:
        engine.dma_start(to, what).then_inc(sem, 16)
    return 16 * len(pairs)


def stream_batches(sp, x_in, x_out, xin, yout, x_loaded, x_used, y_ready, stored, nb, also=None):
    for u in range(2):
        sp.sem_inc(stored[u], 16)
        sp.dma_start(xin[:, u], batch_of(x_in, u)).then_inc(x_loaded[u], 16)
        if also:
            also(u, u)
    with sp.Fori(0, nb // 2 - 1) as i:
        for u in range(2):
            sp.wait_ge(x_used, 2 * i + u + 1)
            sp.dma_start(xin[:, u], batch_of(x_in, 2 * i + u + 2)).then_inc(x_loaded[u], 16)
            if also:
                also(2 * i + u + 2, u)
        for u in range(2):
            sp.wait_ge(y_ready, 2 * i + u + 1)
            sp.dma_start(batch_of(x_out, 2 * i + u), yout[:, u]).then_inc(stored[u], 16)
    for u in range(2):
        sp.wait_ge(y_ready, nb - 2 + u + 1)
        sp.dma_start(batch_of(x_out, nb - 2 + u), yout[:, u]).then_inc(stored[u], 16)
    for u in range(2):
        sp.wait_ge(stored[u], 16 * (nb // 2) + 16)


def tiles(b):
    return b[:].rearrange("p (t d) -> p t d", t=2)


def turn(pe, dst, src, ident):
    for t in range(TT):
        for c in range(DC):
            last = pe.transpose(dst[:, c, t * P:t * P + P], src[:, t, c * P:c * P + P], ident[:])
    return last


def project(pe, dst, wt, src):
    for c in range(DC):
        last = pe.matmul(dst, wt[:, c], src[:, c, :], start=c == 0, stop=c == DC - 1)
    return last


def by_token(pe, dst, src, wt):
    for t in range(TT):
        for c in range(DC):
            last = pe.matmul(dst[:, t, :], src[:, c, t * P:t * P + P], wt[:, c, :],
                             start=c == 0, stop=c == DC - 1)
    return last


PARTS = 3
STACK = 6 * HD


def split(eng, parts, value, rest):
    eng.tensor_tensor(rest, value, parts[:, 0], ALU.subtract)
    eng.drain()
    eng.tensor_copy(parts[:, 1], rest)
    eng.drain()
    return eng.tensor_tensor(parts[:, 2], rest, parts[:, 1], ALU.subtract)


def save_parts(sp, scratch, parts):
    return sp.dma_start(scratch.rearrange("q (c h) e s -> (h e) q c s", c=2), parts)


def stack_q(sp, stack, scratch, sem):
    s = scratch.rearrange("q h e s -> q e h s")
    for row, part, n in ((0, 0, 3), (3, 0, 2), (5, 0, 1)):
        for k in range(n):
            sp.dma_start(stack[(row + k) * HD:(row + k + 1) * HD], s[part + k]).then_inc(sem, 16)


def stack_k(sp, stack, scratch, sem):
    s = scratch.rearrange("q h e s -> q e h s")
    for row, part in enumerate((0, 0, 0, 1, 1, 2)):
        sp.dma_start(stack[row * HD:(row + 1) * HD], s[part]).then_inc(sem, 16)


STACKED = 6 * 16


def distribute(sp, i, q, k, stacked):
    for u in range(2):
        for parts_ready, parts, scratch, saved, _ in (q, k):
            sp.wait_ge(parts_ready, 2 * i + u + 1)
            save_parts(sp, scratch[u], parts[:, u].rearrange("p q (c s) -> p q c s", c=2)).then_inc(saved[u], 16)
    for u in range(2):
        for (_, _, scratch, saved, stack), load in ((q, stack_q), (k, stack_k)):
            sp.wait_ge(saved[u], 16 * (i + 1))
            load(sp, stack[:, u], scratch[u], stacked[u])


def row_stats(dve, src, st, mv, ve):
    for t in range(TT):
        dve.bn_stats(st[:, t, :], src[:, t, :])
    dve.drain()
    for t in range(TT):
        dve.bn_aggr(mv[:, t, :], st[:, t, :])
    dve.drain()
    return dve.tensor_scalar(ve, mv[:, :, 1], LN_EPS, None, ALU.add)


def normalise(dve, out, src, mv, rs):
    return [dve.tensor_scalar(out[:, t, :], src[:, t, :], mv[:, t, 0:1], rs[:, t:t + 1],
                              ALU.subtract, ALU.mult) for t in range(TT)]


def retention_layer(nc, mem, bank, ident_in, x_in, x_out, w, nb):
    def sb(name, shape, dt=F32):
        return mem.enter_context(nc.sbuf_tensor("ret_" + name, [P] + shape, dt))

    def sem(name):
        return nc.alloc_semaphore("ret_" + name)

    ident = sb("ident", [P])
    wq, wk, wv, wg, wo = (sb(n, [DC, D]) for n in ("wq", "wk", "wv", "wg", "wo"))
    w_in, w_out = sb("w_in", [DC, 2, HC, P]), sb("w_out", [HC, D])
    decay = sb("decay", [HEADS, 384])
    cols, rows = sb("cols", [24]), sb("rows", [6, D])
    n1w, n1b, n2w, n2b = (cols[:, 2 * k:2 * k + 2] for k in range(4))
    bq, bk = cols[:, 8:10], cols[:, 10:12]
    bu, bgate = cols[:, 12:18], cols[:, 18:24]
    bv, bg, bo, gn_w, gn_b, b_out = (rows[:, k, :] for k in range(6))

    half = sb("half", [32])
    xin, xhat, xnT = sb("xin", [2, TT, D]), sb("xhat", [2, TT, D]), sb("xnT", [2, DC, SEQ])
    VW = 32
    qf, kf, q_rest, k_rest = (sb(n, [2, DC * SEQ]) for n in ("qf", "kf", "q_rest", "k_rest"))
    q_parts, k_parts = sb("q_parts", [2, PARTS, DC * SEQ], BF16), sb("k_parts", [2, PARTS, DC * SEQ], BF16)
    q_stack, k_stack = sb("q_stack", [2, HEADS, SEQ], BF16), sb("k_stack", [2, HEADS, SEQ], BF16)
    v, gate = sb("v", [2, TT, HEADS, VW]), sb("gate", [2, TT, D])
    rU = sb("rU", [2, GROUPS, SEQ])
    NS = 4
    probs = sb("probs", [NS, 384])
    cen, sq = sb("cen", [2, TT * HEADS, HD]), sb("sq", [2, TT * HEADS, HD])
    s1, s2, s3 = sb("s1", [2, 32]), sb("s2", [2, 32]), sb("s3", [2, 32])
    gated, gT = sb("gated", [2, TT, D]), sb("gT", [2, DC, SEQ])
    x_bo, x1, x_x1 = sb("x_bo", [2, TT, D]), sb("x1", [2, TT, D]), sb("x_x1", [2, TT, D])
    x2T, y = xnT, gated
    hT, su, yout = sb("hT", [2, HC, SEQ]), sb("su", [2, SEQ]), sb("yout", [2, TT, D])
    st, mv = sb("st", [2, TT, 6]), sb("mv", [2, TT, 2])
    ve, rs = sb("ve", [2, 2]), sb("rs", [2, 2])

    scratch = [[nc.dram_tensor(f"ret_{n}_scratch{u}", (PARTS, HEADS, HD, SEQ), BF16, kind="Internal").ap()
                for u in range(2)] for n in "qk"]

    loaded, x_used = sem("loaded"), sem("x_used")
    q_saved, k_saved = [sem(f"q_saved{u}") for u in range(2)], [sem(f"k_saved{u}") for u in range(2)]
    stacked = [sem(f"stacked{u}") for u in range(2)]
    q_split, k_split, rU_ready, rU_turned = sem("q_split"), sem("k_split"), sem("rU_ready"), sem("rU_turned")
    x_loaded = [sem(f"x_loaded{u}") for u in range(2)]
    consts, var1, rstd1, xhat_ready = sem("consts"), sem("var1"), sem("rstd1"), sem("xhat_ready")
    turned, xnT_ready = sem("turned"), sem("xnT_ready")
    q_mm, q_ready, k_mm, k_ready = sem("q_mm"), sem("q_ready"), sem("k_mm"), sem("k_ready")
    v_mm, v_ready, g_mm, g_biased = sem("v_mm"), sem("v_ready"), sem("g_mm"), sem("g_biased")
    gate_ready, s_mm, probs_ready, ret_mm = sem("gate_ready"), sem("s_mm"), sem("probs_ready"), sem("ret_mm")
    cen_ready, sq_ready, gvar, grstd = sem("cen_ready"), sem("sq_ready"), sem("gvar"), sem("grstd")
    gn_ready, gated_ready, gT_mm, gT_ready = sem("gn_ready"), sem("gated_ready"), sem("gT_mm"), sem("gT_ready")
    xbo_ready, o_mm, x1_ready, xx_ready = sem("xbo_ready"), sem("o_mm"), sem("x1_ready"), sem("xx_ready")
    var2, rstd2, xhat2_ready, turned2, x2T_ready = (sem("var2"), sem("rstd2"), sem("xhat2_ready"),
                                                    sem("turned2"), sem("x2T_ready"))
    uv_mm, su_ready, h_ready, out_mm = sem("uv_mm"), sem("su_ready"), sem("h_ready"), sem("out_mm")
    var3, rstd3, y_ready = sem("var3"), sem("rstd3"), sem("y_ready")
    stored = [sem(f"stored{u}") for u in range(2)]

    loads = [(ident[:], ident_in), (cols[:], w["cols"]), (rows[:], w["rows"].partition_broadcast(P)),
             (wq[:], w["wq"]), (wk[:], w["wk"]), (wv[:], w["wv"]), (wg[:], w["wg"]),
             (decay[:], w["decay"]), (wo[:], w["wo"]), (w_in[:], w["w_in"]), (w_out[:], w["w_out"])]

    with nc.Block() as block:
        @block.sync
        def _(sp):
            load_all(sp, loaded, loads)
            for u in range(2):
                sp.sem_inc(stored[u], 16)
                sp.dma_start(xin[:, u], batch_of(x_in, u)).then_inc(x_loaded[u], 16)

            def turn_of_sp(i, more):
                distribute(sp, i, (q_split, q_parts, scratch[0], q_saved, q_stack),
                           (k_split, k_parts, scratch[1], k_saved, k_stack), stacked)
                if more:
                    for u in range(2):
                        sp.wait_ge(x_used, 2 * i + u + 1)
                        sp.dma_start(xin[:, u], batch_of(x_in, 2 * i + u + 2)).then_inc(x_loaded[u], 16)
                for u in range(2):
                    sp.wait_ge(y_ready, 2 * i + u + 1)
                    sp.dma_start(batch_of(x_out, 2 * i + u), yout[:, u]).then_inc(stored[u], 16)

            with sp.Fori(0, nb // 2 - 1) as i:
                turn_of_sp(i, True)
            turn_of_sp(nb // 2 - 1, False)
            for u in range(2):
                sp.wait_ge(stored[u], 16 * (nb // 2) + 16)

        @block.gpsimd
        def _(pool):
            link(pool, pool.memset(half[:], -0.5))
            pool.memset(v[:], 0.0).then_inc(consts, 1)
            pool.wait_ge(loaded, 16 * len(loads))
            with pool.Fori(0, nb // 2) as i:
                for u in range(2):
                    pool.wait_ge(var1, 2 * i + u + 1)
                    pool.tensor_tensor(rs[:, u], ve[:, u], half[:, 0:2], ALU.pow).then_inc(rstd1, 1)
                for u in range(2):
                    pool.wait_ge(k_ready, 2 * i + u + 1)
                    split(pool, k_parts[:, u], kf[:, u], k_rest[:, u]).then_inc(k_split, 1)
                for u in range(2):
                    pool.wait_ge(x_loaded[u], 16 * (i + 1))
                    pool.tensor_tensor(x_bo[:, u], xin[:, u], bo.unsqueeze(1).broadcast_to([P, TT, D]),
                                       ALU.add).then_inc(xbo_ready, 1)
                for u in range(2):
                    pool.wait_ge(gvar, 2 * i + u + 1)
                    pool.tensor_tensor(s3[:, u], s2[:, u], half[:], ALU.pow).then_inc(grstd, 1)
                for u in range(2):
                    pool.wait_ge(gn_ready, 2 * i + u + 1)
                    g, wide = gated[:, u], [P, TT, D]
                    link(pool, pool.tensor_tensor(g, cen[:, u].rearrange("p (t h) e -> p t (h e)", t=TT),
                                               gn_w.unsqueeze(1).broadcast_to(wide), ALU.mult))
                    link(pool, pool.tensor_tensor(g, g, gn_b.unsqueeze(1).broadcast_to(wide), ALU.add))
                    pool.wait_ge(gate_ready, 2 * i + u + 1)
                    pool.tensor_tensor(g, g, gate[:, u], ALU.mult).then_inc(gated_ready, 1)
                for u in range(2):
                    pool.wait_ge(var2, 2 * i + u + 1)
                    pool.tensor_tensor(rs[:, u], ve[:, u], half[:, 0:2], ALU.pow).then_inc(rstd2, 1)
                    link(pool, pool.tensor_tensor(x_x1[:, u], xin[:, u], x1[:, u], ALU.add))
                    pool.tensor_tensor(x_x1[:, u], x_x1[:, u], b_out.unsqueeze(1).broadcast_to([P, TT, D]),
                                       ALU.add).then_inc(xx_ready, 1)
                for u in range(2):
                    pool.wait_ge(var3, 2 * i + u + 1)
                    pool.tensor_tensor(rs[:, u], ve[:, u], half[:, 0:2], ALU.pow).then_inc(rstd3, 1)

        @block.scalar
        def _(act):
            act.wait_ge(loaded, 16 * len(loads))
            with act.Fori(0, nb // 2) as i:
                for u in range(2):
                    for done, b, whole, parts, bias, ready in ((q_mm, 1, qf, q_parts, bq, q_ready),
                                                               (k_mm, 2, kf, k_parts, bk, k_ready)):
                        act.wait_ge(done, 2 * i + u + 1)
                        for out in (whole[:, u], parts[:, u, 0]):
                            for c in range(DC):
                                last = nc.scalar.activation(out[:, c * SEQ:c * SEQ + SEQ],
                                                            tiles(bank[4 * u + b])[:, c, :], ACT.Identity,
                                                            bias=bias[:, c:c + 1])
                        last.then_inc(ready, 1)
                    act.wait_ge(g_biased, 2 * i + u + 1)
                    nc.scalar.activation(gate[:, u], gate[:, u], ACT.Silu).then_inc(gate_ready, 1)
                for u in range(2):
                    act.wait_ge(cen_ready, 2 * i + u + 1)
                    nc.scalar.activation(sq[:, u], cen[:, u], ACT.Square).then_inc(sq_ready, 1)
                for u in range(2):
                    act.wait_ge(gT_mm, 2 * i + u + 1)
                    nc.scalar.activation(gT[:, u], tiles(bank[4 * u + 1]), ACT.Copy).then_inc(gT_ready, 1)
                for u in range(2):
                    for c in range(HC):
                        m = (2 * i + u) * HC + c + 1
                        act.wait_ge(uv_mm, m)
                        if c >= 2:
                            act.wait_ge(h_ready, m - 2)
                        elif u == 1:
                            act.wait_ge(h_ready, m - 2)
                        nc.scalar.activation(su[:, c % 2, :], bank[4 * u + 1 + c % 3][:, 0:256],
                                             ACT.Silu, bias=bu[:, c:c + 1]).then_inc(su_ready, 1)

        @block.vector
        def _(dve):
            dve.wait_ge(loaded, 16 * len(loads))
            with dve.Fori(0, nb // 2) as i:
                for u in range(2):
                    dve.wait_ge(x_loaded[u], 16 * (i + 1))
                    row_stats(dve, xin[:, u], st[:, u], mv[:, u], ve[:, u]).then_inc(var1, 1)
                for u in range(2):
                    dve.wait_ge(rstd1, 2 * i + u + 1)
                    normalise(dve, xhat[:, u], xin[:, u], mv[:, u], rs[:, u])[-1].then_inc(xhat_ready, 1)
                for u in range(2):
                    dve.wait_ge(turned, 2 * i + u + 1)
                    for c in range(DC):
                        last = dve.tensor_scalar(xnT[:, u, c, :], tiles(bank[4 * u])[:, c, :], n1w[:, c:c + 1],
                                                 n1b[:, c:c + 1], ALU.mult, ALU.add)
                    last.then_inc(xnT_ready, 1)
                for u in range(2):
                    dve.wait_ge(v_mm, 2 * i + u + 1)
                    for t in range(TT):
                        last = dve.tensor_tensor(v[:, u, t, :, 0:HD],
                                                 tiles(bank[4 * u + 3])[:, t, :].rearrange("p (h e) -> p h e", e=HD),
                                                 bv.rearrange("p (h e) -> p h e", e=HD), ALU.add)
                    last.then_inc(v_ready, 1)
                    dve.wait_ge(g_mm, 2 * i + u + 1)
                    dve.tensor_tensor(gate[:, u], tiles(bank[4 * u]), bg.unsqueeze(1).broadcast_to([P, TT, D]),
                                      ALU.add).then_inc(g_biased, 1)
                    dve.wait_ge(q_ready, 2 * i + u + 1)
                    split(dve, q_parts[:, u], qf[:, u], q_rest[:, u]).then_inc(q_split, 1)
                for u in range(2):
                    for h in range(HEADS):
                        m = (2 * i + u) * HEADS + h + 1
                        dve.wait_ge(s_mm, m)
                        dve.tensor_tensor(probs[:, h % NS, :], bank[4 * u + 1 + h % 2][:, 0:384],
                                          decay[:, h, :], ALU.mult).then_inc(probs_ready, 1)
                for u in range(2):
                    dve.wait_ge(ret_mm, 2 * i + u + 1)
                    for k in range(2):
                        last = dve.tensor_copy(rU[:, u, 2 * k:2 * k + 2, :], tiles(bank[4 * u + 3 * k]))
                    last.then_inc(rU_ready, 1)
                for u in range(2):
                    dve.wait_ge(rU_turned, 2 * i + u + 1)
                    r = [bank[4 * u + 1 + t][:].rearrange("p (h e) -> p h e", e=VW)[:, :, 0:HD] for t in range(TT)]
                    for t in range(TT):
                        dve.tensor_reduce(s1[:, u, t * HEADS:t * HEADS + HEADS], r[t], AX.X, ALU.add)
                    dve.drain()
                    link(dve, dve.tensor_scalar(s1[:, u], s1[:, u], 1.0 / HD, None, ALU.mult))
                    for t in range(TT):
                        cut = slice(t * HEADS, t * HEADS + HEADS)
                        last = dve.tensor_tensor(cen[:, u, cut], r[t], over(s1[:, u, cut], HD), ALU.subtract)
                    last.then_inc(cen_ready, 1)
                for u in range(2):
                    dve.wait_ge(sq_ready, 2 * i + u + 1)
                    link(dve, dve.tensor_reduce(s2[:, u], sq[:, u], AX.X, ALU.add))
                    dve.tensor_scalar(s2[:, u], s2[:, u], 1.0 / HD, LN_EPS, ALU.mult, ALU.add).then_inc(gvar, 1)
                for u in range(2):
                    dve.wait_ge(grstd, 2 * i + u + 1)
                    dve.tensor_tensor(cen[:, u], cen[:, u], over(s3[:, u], HD), ALU.mult).then_inc(gn_ready, 1)
                for u in range(2):
                    dve.wait_ge(o_mm, 2 * i + u + 1)
                    dve.wait_ge(xbo_ready, 2 * i + u + 1)
                    dve.tensor_tensor(x1[:, u], tiles(bank[4 * u + 2]), x_bo[:, u], ALU.add).then_inc(x1_ready, 1)
                    dve.wait_ge(x1_ready, 2 * i + u + 1)
                    row_stats(dve, x1[:, u], st[:, u], mv[:, u], ve[:, u]).then_inc(var2, 1)
                for u in range(2):
                    dve.wait_ge(rstd2, 2 * i + u + 1)
                    normalise(dve, xhat[:, u], x1[:, u], mv[:, u], rs[:, u])[-1].then_inc(xhat2_ready, 1)
                for u in range(2):
                    dve.wait_ge(turned2, 2 * i + u + 1)
                    for c in range(DC):
                        last = dve.tensor_scalar(x2T[:, u, c, :], tiles(bank[4 * u])[:, c, :], n2w[:, c:c + 1],
                                                 n2b[:, c:c + 1], ALU.mult, ALU.add)
                    last.then_inc(x2T_ready, 1)
                for u in range(2):
                    for c in range(HC):
                        dve.wait_ge(su_ready, (2 * i + u) * HC + c + 1)
                        dve.scalar_tensor_tensor(out=hT[:, u, c, :], in0=bank[4 * u + 1 + c % 3][:, 256:512],
                                                 scalar=bgate[:, c:c + 1], in1=su[:, c % 2, :],
                                                 op0=ALU.add, op1=ALU.mult).then_inc(h_ready, 1)
                for u in range(2):
                    dve.wait_ge(out_mm, 2 * i + u + 1)
                    dve.wait_ge(xx_ready, 2 * i + u + 1)
                    dve.tensor_tensor(y[:, u], tiles(bank[4 * u]), x_x1[:, u], ALU.add).then_inc(x_used, 1)
                    dve.wait_ge(x_used, 2 * i + u + 1)
                    row_stats(dve, y[:, u], st[:, u], mv[:, u], ve[:, u]).then_inc(var3, 1)
                for u in range(2):
                    dve.wait_ge(rstd3, 2 * i + u + 1)
                    dve.wait_ge(stored[u], 16 * (i + 1))
                    normalise(dve, yout[:, u], y[:, u], mv[:, u], rs[:, u])[-1].then_inc(y_ready, 1)

        @block.tensor
        def _(pe):
            pe.wait_ge(loaded, 16 * len(loads))
            pe.wait_ge(consts, 1)

            with pe.Fori(0, nb // 2) as i:
                for u in range(2):
                    pe.wait_ge(xhat_ready, 2 * i + u + 1)
                    turn(pe, tiles(bank[4 * u]), xhat[:, u], ident).then_inc(turned, 1)
                for u in range(2):
                    n = 2 * i + u
                    pe.wait_ge(xnT_ready, n + 1)
                    x = xnT[:, u]
                    for wt, b, done in ((wq, 1, q_mm), (wk, 2, k_mm)):
                        for g in range(2):
                            last = project(pe, tiles(bank[4 * u + b])[:, g], wt[:, :, g * P:g * P + P], x)
                        last.then_inc(done, 1)
                    by_token(pe, tiles(bank[4 * u + 3]), x, wv).then_inc(v_mm, 1)
                    by_token(pe, tiles(bank[4 * u]), x, wg).then_inc(g_mm, 1)

                for u in range(2):
                    n = 2 * i + u

                    def scores(h):
                        if h == 0:
                            pe.wait_ge(stacked[u], 2 * STACKED * (i + 1))
                            pe.wait_ge(g_biased, n + 1)
                        if h >= 2:
                            pe.wait_ge(probs_ready, n * HEADS + h - 1)
                        for t in range(TT):
                            last = pe.matmul(bank[4 * u + 1 + h % 2][:, 256 * t:256 * t + 256 - P * t],
                                             k_stack[0:STACK, u, h, t * P:t * P + P],
                                             q_stack[0:STACK, u, h, t * P:SEQ], start=True, stop=True)
                        last.then_inc(s_mm, 1)

                    def values(h):
                        g, j = h // 4, 32 * (h % 4)
                        pe.wait_ge(probs_ready, n * HEADS + h + 1)
                        r = tiles(bank[4 * u + 3 * (g // 2)])[j:j + VW, g % 2, :]
                        pe.matmul(r, v[:, u, 0, h, :], probs[:, h % NS, 0:256], start=True, stop=False)
                        return pe.matmul(r[:, P:256], v[:, u, 1, h, :], probs[:, h % NS, 256:384],
                                         start=False, stop=True)

                    for h in range(HEADS + 1):
                        if h < HEADS:
                            scores(h)
                        if h >= 1:
                            last = values(h - 1)
                    last.then_inc(ret_mm, 1)
                for u in range(2):
                    pe.wait_ge(rU_ready, 2 * i + u + 1)
                    for t in range(TT):
                        for g in range(GROUPS):
                            last = pe.transpose(bank[4 * u + 1 + t][:, g * P:g * P + P],
                                                rU[:, u, g, t * P:t * P + P], ident[:])
                    last.then_inc(rU_turned, 1)
                for u in range(2):
                    pe.wait_ge(gated_ready, 2 * i + u + 1)
                    turn(pe, tiles(bank[4 * u + 1]), gated[:, u], ident).then_inc(gT_mm, 1)
                for u in range(2):
                    pe.wait_ge(gT_ready, 2 * i + u + 1)
                    by_token(pe, tiles(bank[4 * u + 2]), gT[:, u], wo).then_inc(o_mm, 1)
                for u in range(2):
                    pe.wait_ge(xhat2_ready, 2 * i + u + 1)
                    turn(pe, tiles(bank[4 * u]), xhat[:, u], ident).then_inc(turned2, 1)
                for u in range(2):
                    n = 2 * i + u
                    pe.wait_ge(x2T_ready, n + 1)
                    for c in range(HC):
                        if c >= 3:
                            pe.wait_ge(h_ready, n * HC + c - 2)
                        b = tiles(bank[4 * u + 1 + c % 3])
                        for half_w in range(2):
                            last = project(pe, b[:, half_w, :], w_in[:, :, half_w, c, :], x2T[:, u])
                        last.then_inc(uv_mm, 1)
                for u in range(2):
                    n = 2 * i + u
                    pe.wait_ge(h_ready, n * HC + HC)
                    for t in range(TT):
                        for c in range(HC):
                            last = pe.matmul(tiles(bank[4 * u])[:, t, :], hT[:, u, c, t * P:t * P + P], w_out[:, c, :],
                                      start=c == 0, stop=c == HC - 1)
                    last.then_inc(out_mm, 1)


def cross_attention_layer(nc, mem, bank, ident_in, x_in, x_out, w, nb):
    def sb(name, shape, dt=F32):
        return mem.enter_context(nc.sbuf_tensor("xat_" + name, [P] + shape, dt))

    def sem(name):
        return nc.alloc_semaphore("xat_" + name)

    ident, ident16 = sb("ident", [P]), sb("ident16", [P], BF16)
    wq, wk, wv, wo = (sb(n, [DC, D]) for n in ("wq", "wk", "wv", "wo"))
    cols, rows = sb("cols", [4]), sb("rows", [2, D])
    bq, bk = cols[:, 0:2], cols[:, 2:4]
    bv, bo = rows[:, 0, :], rows[:, 1, :]
    bq_scaled = sb("bq_scaled", [2])
    SCALE = HD ** -0.5
    VW = 32
    FULL = STACK + PARTS

    half, neg = sb("half", [2]), sb("neg", [32])
    xin, cT, xT = sb("xin", [2, TT, D]), sb("cT", [2, DC, SEQ]), sb("xT", [2, DC, SEQ])
    qf, kf, q_rest, k_rest = (sb(n, [2, DC * SEQ]) for n in ("qf", "kf", "q_rest", "k_rest"))
    q_parts, k_parts = sb("q_parts", [2, PARTS, DC * SEQ], BF16), sb("k_parts", [2, PARTS, DC * SEQ], BF16)
    q_stack, k_stack = sb("q_stack", [2, HEADS, SEQ], BF16), sb("k_stack", [2, HEADS, SEQ], BF16)
    v = sb("v", [2, TT, HEADS, VW])
    mx, nmx, nmx_rest = sb("mx", [2, TT, HEADS]), sb("nmx", [2, TT * HEADS]), sb("nmx_rest", [2, TT * HEADS])
    nmx_parts, nmxT = sb("nmx_parts", [2, PARTS, TT * HEADS], BF16), sb("nmxT", [2, P], BF16)
    NS = 4
    probs = sb("probs", [NS, TT, SEQ])
    oU, rsum = sb("oU", [2, GROUPS, SEQ]), sb("rsum", [2, TT, HEADS])
    o, oT = sb("o", [2, TT, D]), sb("oT", [2, DC, SEQ])
    x_bo, y, yout = sb("x_bo", [2, TT, D]), sb("y", [2, TT, D]), sb("yout", [2, TT, D])
    st, mv, ve, rs = sb("st", [2, TT, 6]), sb("mv", [2, TT, 2]), sb("ve", [2, 2]), sb("rs", [2, 2])
    scratch = [[nc.dram_tensor(f"xat_{n}_scratch{u}", (PARTS, HEADS, HD, SEQ), BF16, kind="Internal").ap()
                for u in range(2)] for n in "qk"]

    loaded, x_used, consts = sem("loaded"), sem("x_used"), sem("consts")
    x_loaded, c_loaded = [sem(f"x_loaded{u}") for u in range(2)], [sem(f"c_loaded{u}") for u in range(2)]
    stored = [sem(f"stored{u}") for u in range(2)]
    q_saved, k_saved = [sem(f"q_saved{u}") for u in range(2)], [sem(f"k_saved{u}") for u in range(2)]
    stacked, nmx_placed = [sem(f"stacked{u}") for u in range(2)], [sem(f"nmx_placed{u}") for u in range(2)]
    turned, xT_ready, q_mm, k_mm, v_mm = sem("turned"), sem("xT_ready"), sem("q_mm"), sem("k_mm"), sem("v_mm")
    q_ready, k_ready, q_split, k_split, v_ready = (sem("q_ready"), sem("k_ready"), sem("q_split"),
                                                   sem("k_split"), sem("v_ready"))
    sq_mm, max_taken, nmx_ready, nmx_turned, nmxT_ready = (sem("sq_mm"), sem("max_taken"), sem("nmx_ready"),
                                                           sem("nmx_turned"), sem("nmxT_ready"))
    sk_mm, probs_ready, values_done, oU_ready, oU_turned = (sem("sk_mm"), sem("probs_ready"), sem("values_done"),
                                                            sem("oU_ready"), sem("oU_turned"))
    o_ready, o_turned, oT_ready = sem("o_ready"), sem("o_turned"), sem("oT_ready")
    xbo_ready, o_mm, var, rstd, y_ready = sem("xbo_ready"), sem("o_mm"), sem("var"), sem("rstd"), sem("y_ready")

    loads = [(ident[:], ident_in), (cols[:], w["cols"]), (rows[:], w["rows"].partition_broadcast(P)),
             (wq[:], w["wq"]), (wk[:], w["wk"]), (wv[:], w["wv"]), (wo[:], w["wo"])]

    def context(n):
        return w["contextT"][bass.ds(n, 1)].rearrange("a (c p) s -> p (a c) s", p=P)

    with nc.Block() as block:
        @block.sync
        def _(sp):
            load_all(sp, loaded, loads)
            for u in range(2):
                sp.sem_inc(stored[u], 16)
                sp.dma_start(xin[:, u], batch_of(x_in, u)).then_inc(x_loaded[u], 16)
                sp.dma_start(cT[:, u], context(u)).then_inc(c_loaded[u], 16)

            def turn_of_sp(i, more):
                distribute(sp, i, (q_split, q_parts, scratch[0], q_saved, q_stack),
                           (k_split, k_parts, scratch[1], k_saved, k_stack), stacked)
                if more:
                    for u in range(2):
                        sp.wait_ge(v_mm, 2 * i + u + 1)
                        sp.dma_start(cT[:, u], context(2 * i + u + 2)).then_inc(c_loaded[u], 16)
                for u in range(2):
                    sp.wait_ge(nmxT_ready, 2 * i + u + 1)
                    for k in range(PARTS):
                        for t in range(TT):
                            row = k * 32 + t * HEADS
                            sp.dma_start(q_stack[STACK + k:STACK + k + 1, u, :, t * P:t * P + P],
                                         nmxT[row:row + HEADS, u, :]).then_inc(nmx_placed[u], 16)
                if more:
                    for u in range(2):
                        sp.wait_ge(x_used, 2 * i + u + 1)
                        sp.dma_start(xin[:, u], batch_of(x_in, 2 * i + u + 2)).then_inc(x_loaded[u], 16)
                for u in range(2):
                    sp.wait_ge(y_ready, 2 * i + u + 1)
                    sp.dma_start(batch_of(x_out, 2 * i + u), yout[:, u]).then_inc(stored[u], 16)

            with sp.Fori(0, nb // 2 - 1) as i:
                turn_of_sp(i, True)
            turn_of_sp(nb // 2 - 1, False)
            for u in range(2):
                sp.wait_ge(stored[u], 16 * (nb // 2) + 16)

        @block.gpsimd
        def _(pool):
            pool.memset(half[:], -0.5)
            pool.memset(neg[:], -1.0)
            pool.memset(v[:], 1.0)
            pool.drain()
            pool.memset(k_stack[STACK:STACK + 32], 1.0)
            pool.drain()
            pool.wait_ge(loaded, 16 * len(loads))
            pool.tensor_copy(ident16[:], ident[:])
            pool.drain()
            pool.tensor_scalar(bq_scaled[:], bq, SCALE, None, ALU.mult).then_inc(consts, 1)
            with pool.Fori(0, nb // 2) as i:
                for u in range(2):
                    pool.wait_ge(k_ready, 2 * i + u + 1)
                    split(pool, k_parts[:, u], kf[:, u], k_rest[:, u]).then_inc(k_split, 1)
                for u in range(2):
                    pool.wait_ge(x_loaded[u], 16 * (i + 1))
                    pool.tensor_tensor(x_bo[:, u], xin[:, u], bo.unsqueeze(1).broadcast_to([P, TT, D]),
                                       ALU.add).then_inc(xbo_ready, 1)
                for u in range(2):
                    pool.wait_ge(max_taken, (2 * i + u + 1) * 16)
                    pool.tensor_tensor(nmx[:, u], mx[:, u].rearrange("p t h -> p (t h)"), neg[:], ALU.mult)
                    pool.drain()
                    pool.tensor_copy(nmx_parts[:, u, 0], nmx[:, u])
                    pool.drain()
                    split(pool, nmx_parts[:, u], nmx[:, u], nmx_rest[:, u]).then_inc(nmx_ready, 1)
                for u in range(2):
                    pool.wait_ge(var, 2 * i + u + 1)
                    pool.tensor_tensor(rs[:, u], ve[:, u], half[:], ALU.pow).then_inc(rstd, 1)

        @block.scalar
        def _(act):
            act.wait_ge(loaded, 16 * len(loads))
            act.wait_ge(consts, 1)
            with act.Fori(0, nb // 2) as i:
                for u in range(2):
                    act.wait_ge(turned, 2 * i + u + 1)
                    nc.scalar.activation(xT[:, u], tiles(bank[4 * u]), ACT.Copy).then_inc(xT_ready, 1)
                for u in range(2):
                    for done, b, whole, parts, bias, scale, ready in (
                            (k_mm, 2, kf, k_parts, bk, 1.0, k_ready),
                            (q_mm, 1, qf, q_parts, bq_scaled, SCALE, q_ready)):
                        act.wait_ge(done, 2 * i + u + 1)
                        for out in (whole[:, u], parts[:, u, 0]):
                            for c in range(DC):
                                last = nc.scalar.activation(out[:, c * SEQ:c * SEQ + SEQ],
                                                            tiles(bank[4 * u + b])[:, c, :], ACT.Identity,
                                                            bias=bias[:, c:c + 1], scale=scale)
                        last.then_inc(ready, 1)
                for u in range(2):
                    act.wait_ge(nmx_turned, 2 * i + u + 1)
                    nc.scalar.activation(nmxT[0:96, u, :], bank[4 * u][0:96, 0:P // 2].bitcast(BF16),
                                         ACT.Copy).then_inc(nmxT_ready, 1)
                for u in range(2):
                    for h in range(HEADS):
                        m = (2 * i + u) * HEADS + h + 1
                        act.wait_ge(sk_mm, m)
                        nc.scalar.activation(probs[:, h % NS], tiles(bank[4 * u + 1 + h % 2]), ACT.Exp)\
                            .then_inc(probs_ready, 1)
                for u in range(2):
                    act.wait_ge(o_turned, 2 * i + u + 1)
                    nc.scalar.activation(oT[:, u], tiles(bank[4 * u + 1]), ACT.Copy).then_inc(oT_ready, 1)

        @block.vector
        def _(dve):
            dve.wait_ge(loaded, 16 * len(loads))
            dve.wait_ge(consts, 1)
            with dve.Fori(0, nb // 2) as i:
                for u in range(2):
                    dve.wait_ge(q_ready, 2 * i + u + 1)
                    split(dve, q_parts[:, u], qf[:, u], q_rest[:, u]).then_inc(q_split, 1)
                    dve.wait_ge(v_mm, 2 * i + u + 1)
                    for t in range(TT):
                        last = dve.tensor_tensor(v[:, u, t, :, 0:HD],
                                                 tiles(bank[4 * u + 3])[:, t, :].rearrange("p (h e) -> p h e", e=HD),
                                                 bv.rearrange("p (h e) -> p h e", e=HD), ALU.add)
                    last.then_inc(v_ready, 1)
                for u in range(2):
                    for m in range(16):
                        t, h = m // 8, m % 8 * 2
                        dve.wait_ge(sq_mm, (2 * i + u) * 16 + m + 1)
                        dve.tensor_reduce(mx[:, u, t, h:h + 2], tiles(bank[4 * u + m % 4]), AX.X, ALU.max)\
                           .then_inc(max_taken, 1)
                for u in range(2):
                    dve.wait_ge(values_done, 2 * i + u + 1)
                    for k in range(2):
                        last = dve.tensor_copy(oU[:, u, 2 * k:2 * k + 2, :], tiles(bank[4 * u + 3 * k]))
                    last.then_inc(oU_ready, 1)
                for u in range(2):
                    dve.wait_ge(oU_turned, 2 * i + u + 1)
                    for t in range(TT):
                        s = bank[4 * u + 1 + t][:].rearrange("p (h e) -> p h e", e=VW)
                        dve.reciprocal(rsum[:, u, t], s[:, :, HD])
                        dve.drain()
                        last = dve.tensor_tensor(o[:, u, t].rearrange("p (h e) -> p h e", e=HD), s[:, :, 0:HD],
                                                 over(rsum[:, u, t], HD), ALU.mult)
                    last.then_inc(o_ready, 1)
                for u in range(2):
                    dve.wait_ge(o_mm, 2 * i + u + 1)
                    dve.wait_ge(xbo_ready, 2 * i + u + 1)
                    dve.tensor_tensor(y[:, u], tiles(bank[4 * u + 2]), x_bo[:, u], ALU.add).then_inc(x_used, 1)
                    dve.drain()
                    row_stats(dve, y[:, u], st[:, u], mv[:, u], ve[:, u]).then_inc(var, 1)
                for u in range(2):
                    dve.wait_ge(rstd, 2 * i + u + 1)
                    dve.wait_ge(stored[u], 16 * (i + 1))
                    normalise(dve, yout[:, u], y[:, u], mv[:, u], rs[:, u])[-1].then_inc(y_ready, 1)

        @block.tensor
        def _(pe):
            pe.wait_ge(loaded, 16 * len(loads))
            pe.wait_ge(consts, 1)
            with pe.Fori(0, nb // 2) as i:
                for u in range(2):
                    n = 2 * i + u
                    pe.wait_ge(x_loaded[u], 16 * (i + 1))
                    turn(pe, tiles(bank[4 * u]), xin[:, u], ident).then_inc(turned, 1)
                    pe.wait_ge(c_loaded[u], 16 * (i + 1))
                    for g in range(2):
                        last = project(pe, tiles(bank[4 * u + 2])[:, g], wk[:, :, g * P:g * P + P], cT[:, u])
                    last.then_inc(k_mm, 1)
                    by_token(pe, tiles(bank[4 * u + 3]), cT[:, u], wv).then_inc(v_mm, 1)
                    pe.wait_ge(xT_ready, n + 1)
                    for g in range(2):
                        last = project(pe, tiles(bank[4 * u + 1])[:, g], wq[:, :, g * P:g * P + P], xT[:, u])
                    last.then_inc(q_mm, 1)
                for u in range(2):
                    n = 2 * i + u
                    pe.wait_ge(stacked[u], 2 * STACKED * (i + 1))
                    pe.wait_ge(v_ready, n + 1)
                    for m in range(16):
                        t, h = m // 8, m % 8 * 2
                        if m >= 4:
                            pe.wait_ge(max_taken, n * 16 + m - 3)
                        for k in range(2):
                            last = pe.matmul(bank[4 * u + m % 4][:, 256 * k:256 * k + 256],
                                             q_stack[0:STACK, u, h + k, t * P:t * P + P],
                                             k_stack[0:STACK, u, h + k, :], start=True, stop=True)
                        last.then_inc(sq_mm, 1)
                for u in range(2):
                    n = 2 * i + u
                    pe.wait_ge(nmx_ready, n + 1)
                    for k in range(PARTS):
                        last = pe.transpose(bank[4 * u][32 * k:32 * k + 32, 0:P // 2].bitcast(BF16),
                                            nmx_parts[:, u, k, :], ident16[:])
                    last.then_inc(nmx_turned, 1)
                for u in range(2):
                    n = 2 * i + u

                    def scores(h):
                        if h == 0:
                            pe.wait_ge(nmx_placed[u], PARTS * TT * 16 * (i + 1))
                            pe.wait_ge(max_taken, (n + 1) * 16)
                        if h >= 2:
                            pe.wait_ge(probs_ready, n * HEADS + h - 1)
                        for c in range(TT):
                            last = pe.matmul(bank[4 * u + 1 + h % 2][:, 256 * c:256 * c + 256],
                                             k_stack[0:FULL, u, h, c * P:c * P + P], q_stack[0:FULL, u, h, :],
                                             start=True, stop=True)
                        last.then_inc(sk_mm, 1)

                    def values(h):
                        g, j = h // 4, 32 * (h % 4)
                        pe.wait_ge(probs_ready, n * HEADS + h + 1)
                        for c in range(TT):
                            last = pe.matmul(bank[4 * u + 3 * (g // 2)][j:j + VW, g % 2 * 256:g % 2 * 256 + 256],
                                             v[:, u, c, h, :], probs[:, h % NS, c, :], start=c == 0, stop=c == TT - 1)
                        return last

                    for h in range(HEADS + 1):
                        if h < HEADS:
                            scores(h)
                        if h >= 1:
                            last = values(h - 1)
                    last.then_inc(values_done, 1)
                for u in range(2):
                    pe.wait_ge(oU_ready, 2 * i + u + 1)
                    for t in range(TT):
                        for g in range(GROUPS):
                            last = pe.transpose(bank[4 * u + 1 + t][:, g * P:g * P + P],
                                                oU[:, u, g, t * P:t * P + P], ident[:])
                    last.then_inc(oU_turned, 1)
                for u in range(2):
                    pe.wait_ge(o_ready, 2 * i + u + 1)
                    turn(pe, tiles(bank[4 * u + 1]), o[:, u], ident).then_inc(o_turned, 1)
                for u in range(2):
                    pe.wait_ge(oT_ready, 2 * i + u + 1)
                    by_token(pe, tiles(bank[4 * u + 2]), oT[:, u], wo).then_inc(o_mm, 1)


def channel_mix_layer(nc, mem, bank, ident_in, x_in, x_out, w, nb):
    def sb(name, shape, dt=F32):
        return mem.enter_context(nc.sbuf_tensor("mix_" + name, [P] + shape, dt))

    def sem(name):
        return nc.alloc_semaphore("mix_" + name)

    ident = sb("ident", [P])
    wr, wk, wv = sb("wr", [DC, D]), sb("wk", [DC, D]), sb("wv", [DC, D])
    mu, mu_rest = sb("mu", [4]), sb("mu_rest", [4])
    half = sb("half", [2])
    xin, shifted = sb("xin", [2, TT, D]), sb("shifted", [2, DC, SEQ + 1])
    before, mixed = sb("before", [2, 2, DC, SEQ]), sb("mixed", [2, 2, DC, SEQ])
    r, relu_k, k_act = sb("r", [2, TT, D]), sb("relu_k", [2, DC, SEQ]), sb("k_act", [2, DC, SEQ])
    y, yout = sb("y", [2, TT, D]), sb("yout", [2, TT, D])
    st, mv, ve, rs = sb("st", [2, TT, 6]), sb("mv", [2, TT, 2]), sb("ve", [2, 2]), sb("rs", [2, 2])

    loaded, x_used, consts = sem("loaded"), sem("x_used"), sem("consts")
    x_loaded, stored = [sem(f"x_loaded{u}") for u in range(2)], [sem(f"stored{u}") for u in range(2)]
    turned, xT_ready, before_ready, mixed_ready = (sem("turned"), sem("xT_ready"), sem("before_ready"),
                                                   sem("mixed_ready"))
    r_mm, r_ready, k_mm, relu_ready, k_act_ready = (sem("r_mm"), sem("r_ready"), sem("k_mm"),
                                                    sem("relu_ready"), sem("k_act_ready"))
    v_mm, var, rstd, y_ready = sem("v_mm"), sem("var"), sem("rstd"), sem("y_ready")

    loads = [(ident[:], ident_in), (mu[:], w["mu"]), (wr[:], w["wr"]), (wk[:], w["wk"]), (wv[:], w["wv"])]

    with nc.Block() as block:
        @block.sync
        def _(sp):
            load_all(sp, loaded, loads)
            stream_batches(sp, x_in, x_out, xin, yout, x_loaded, x_used, y_ready, stored, nb)

        @block.gpsimd
        def _(pool):
            pool.memset(half[:], -0.5)
            pool.memset(shifted[:], 0.0)
            pool.drain()
            pool.wait_ge(loaded, 16 * len(loads))
            pool.tensor_scalar(mu_rest[:], mu[:], -1.0, 1.0, ALU.mult, ALU.add).then_inc(consts, 1)
            with pool.Fori(0, nb // 2) as i:
                for u in range(2):
                    pool.wait_ge(var, 2 * i + u + 1)
                    pool.tensor_tensor(rs[:, u], ve[:, u], half[:], ALU.pow).then_inc(rstd, 1)

        @block.scalar
        def _(act):
            act.wait_ge(loaded, 16 * len(loads))
            act.wait_ge(consts, 1)
            with act.Fori(0, nb // 2) as i:
                for u in range(2):
                    act.wait_ge(turned, 2 * i + u + 1)
                    nc.scalar.activation(shifted[:, u, :, 1:SEQ + 1], tiles(bank[4 * u]), ACT.Copy)\
                        .then_inc(xT_ready, 1)
                for u in range(2):
                    act.wait_ge(xT_ready, 2 * i + u + 1)
                    for k in range(2):
                        for c in range(DC):
                            last = nc.scalar.activation(before[:, u, k, c, :], shifted[:, u, c, 0:SEQ], ACT.Copy,
                                                        scale=mu_rest[:, 2 * k + c:2 * k + c + 1])
                    last.then_inc(before_ready, 1)
                for u in range(2):
                    act.wait_ge(k_mm, 2 * i + u + 1)
                    nc.scalar.activation(relu_k[:, u], tiles(bank[4 * u + 2]), ACT.Relu).then_inc(relu_ready, 1)
                    act.wait_ge(r_mm, 2 * i + u + 1)
                    nc.scalar.activation(r[:, u], tiles(bank[4 * u + 1]), ACT.Sigmoid).then_inc(r_ready, 1)

        @block.vector
        def _(dve):
            dve.wait_ge(loaded, 16 * len(loads))
            with dve.Fori(0, nb // 2) as i:
                for u in range(2):
                    dve.wait_ge(before_ready, 2 * i + u + 1)
                    for k in range(2):
                        for c in range(DC):
                            last = dve.scalar_tensor_tensor(
                                out=mixed[:, u, k, c, :], in0=shifted[:, u, c, 1:SEQ + 1],
                                scalar=mu[:, 2 * k + c:2 * k + c + 1], in1=before[:, u, k, c, :],
                                op0=ALU.mult, op1=ALU.add)
                    last.then_inc(mixed_ready, 1)
                for u in range(2):
                    dve.wait_ge(relu_ready, 2 * i + u + 1)
                    dve.scalar_tensor_tensor(out=k_act[:, u], in0=tiles(bank[4 * u + 2]), scalar=0.0,
                                             in1=relu_k[:, u], op0=ALU.max, op1=ALU.mult).then_inc(k_act_ready, 1)
                for u in range(2):
                    dve.wait_ge(r_ready, 2 * i + u + 1)
                    dve.wait_ge(v_mm, 2 * i + u + 1)
                    dve.tensor_tensor(y[:, u], tiles(bank[4 * u + 3]), r[:, u], ALU.mult)
                    dve.drain()
                    dve.tensor_tensor(y[:, u], y[:, u], xin[:, u], ALU.add).then_inc(x_used, 1)
                    dve.drain()
                    row_stats(dve, y[:, u], st[:, u], mv[:, u], ve[:, u]).then_inc(var, 1)
                for u in range(2):
                    dve.wait_ge(rstd, 2 * i + u + 1)
                    dve.wait_ge(stored[u], 16 * (i + 1))
                    normalise(dve, yout[:, u], y[:, u], mv[:, u], rs[:, u])[-1].then_inc(y_ready, 1)

        @block.tensor
        def _(pe):
            pe.wait_ge(loaded, 16 * len(loads))
            with pe.Fori(0, nb // 2) as i:
                for u in range(2):
                    pe.wait_ge(x_loaded[u], 16 * (i + 1))
                    turn(pe, tiles(bank[4 * u]), xin[:, u], ident).then_inc(turned, 1)
                for u in range(2):
                    pe.wait_ge(mixed_ready, 2 * i + u + 1)
                    for g in range(DC):
                        last = project(pe, tiles(bank[4 * u + 2])[:, g], wk[:, :, g * P:g * P + P], mixed[:, u, 1])
                    last.then_inc(k_mm, 1)
                    by_token(pe, tiles(bank[4 * u + 1]), mixed[:, u, 0], wr).then_inc(r_mm, 1)
                for u in range(2):
                    pe.wait_ge(k_act_ready, 2 * i + u + 1)
                    by_token(pe, tiles(bank[4 * u + 3]), k_act[:, u], wv).then_inc(v_mm, 1)


def relative_attention_layer(nc, mem, bank, ident_in, x_in, x_out, w, nb):
    def sb(name, shape, dt=F32):
        return mem.enter_context(nc.sbuf_tensor("rel_" + name, [P] + shape, dt))

    def sem(name):
        return nc.alloc_semaphore("rel_" + name)

    A = P // HEADS
    TILES = SEQ // A
    UNITS = TILES // 2
    SPAN = SEQ + TILES - 1
    SHIFTS = SEQ + P
    BLK = HEADS + A
    SCALE = HD ** -0.5

    ident, half = sb("ident", [P]), sb("half", [2])
    wq, wk, wv, wo = (sb(n, [DC, D]) for n in ("wq", "wk", "wv", "wo"))
    cols, rows = sb("cols", [4]), sb("rows", [2, D])
    bq, bk = cols[:, 0:2], cols[:, 2:4]
    bv, bo = rows[:, 0, :], rows[:, 1, :]
    bq_scaled = sb("bq_scaled", [2])
    mask_h, mask_a, own = sb("mask_h", [DC, HEADS]), sb("mask_a", [A]), sb("own", [BLK])
    dist_k, dist_v = sb("dist_k", [SPAN]), sb("dist_v", [SHIFTS, HD])

    xin, xT = sb("xin", [2, TT, D]), sb("xT", [2, DC, SEQ])
    qT, kT, v = sb("qT", [2, DC, SEQ]), sb("kT", [2, DC, SEQ]), sb("v", [2, TT, D])
    q_by_a = sb("q_by_a", [2, HEADS, TILES])
    q_wide, q_dist = sb("q_wide", [2, DC, TILES, P]), sb("q_dist", [2, TILES, P])
    probs, pT = sb("probs", [2, 2, SEQ]), sb("pT", [2, 2, TT, P])
    mx, nmx, sums = sb("mx", [TILES]), sb("nmx", [TILES]), sb("sums", [2, TILES])
    kept = sb("kept", [2, BLK, HD])
    out, rsum = sb("out", [2, TILES, HD]), sb("rsum", [TILES])
    o, oT = sb("o", [2, TT, D]), sb("oT", [2, DC, SEQ])
    x_bo, yout = sb("x_bo", [2, TT, D]), sb("yout", [2, TT, D])
    st, mv, ve, rs = sb("st", [2, TT, 6]), sb("mv", [2, TT, 2]), sb("ve", [2, 2]), sb("rs", [2, 2])
    q_scratch = [nc.dram_tensor(f"rel_q_scratch{u}", (HEADS, HD, SEQ), F32, kind="Internal").ap() for u in range(2)]
    o_scratch = [nc.dram_tensor(f"rel_o_scratch{u}", (SEQ, D), F32, kind="Internal").ap() for u in range(2)]

    loaded, x_used, consts = sem("loaded"), sem("x_used"), sem("consts")
    x_loaded, stored, q_saved, q_relaid, o_saved, o_loaded = (
        [sem(f"{n}{u}") for u in range(2)]
        for n in ("x_loaded", "stored", "q_saved", "q_relaid", "o_saved", "o_loaded"))
    turned, xT_ready, q_mm, k_mm, v_mm = sem("turned"), sem("xT_ready"), sem("q_mm"), sem("k_mm"), sem("v_mm")
    q_ready, k_ready, v_ready, wide_ready = sem("q_ready"), sem("k_ready"), sem("v_ready"), sem("wide_ready")
    scores_mm, max_ready, probs_ready, probs_turned, pT_ready = (
        sem("scores_mm"), sem("max_ready"), sem("probs_ready"), sem("probs_turned"), sem("pT_ready"))
    values_mm, kept_ready, out_ready = sem("values_mm"), sem("kept_ready"), sem("out_ready")
    o_turned, oT_ready, o_mm, xbo_ready = sem("o_turned"), sem("oT_ready"), sem("o_mm"), sem("xbo_ready")
    var, rstd, y_ready = sem("var"), sem("rstd"), sem("y_ready")

    PART_TILES = 8
    PARTS_Q = TILES // PART_TILES

    loads = [(ident[:], ident_in), (cols[:], w["cols"]), (rows[:], w["rows"].partition_broadcast(P)),
             (wq[:], w["wq"]), (wk[:], w["wk"]), (wv[:], w["wv"]), (wo[:], w["wo"]),
             (mask_h[:], w["mask_h"]), (mask_a[:], w["mask_a"]), (own[:], w["own"])]
    at = w["ext_kT"].shape[1] // 2 - (TILES - 1)
    loads += [(dist_k[a * HD:a * HD + HD], w["ext_kT"][:, at - TILES * a:at - TILES * a + SPAN]) for a in range(A)]
    first = w["ext_v"].shape[0] // 2 - (SEQ - 1)
    loads += [(dist_v[:], bass.AP(w["ext_v"].tensor, first * HD, [[HD, P], [HD, SHIFTS], [1, HD]]))]

    with nc.Block() as block:
        @block.sync
        def _(sp):
            load_all(sp, loaded, loads)
            for u in range(2):
                sp.sem_inc(stored[u], 16)
                sp.dma_start(xin[:, u], batch_of(x_in, u)).then_inc(x_loaded[u], 16)

            def turn_of_sp(i, more):
                for u in range(2):
                    sp.wait_ge(q_ready, 2 * i + u + 1)
                    sp.dma_start(q_scratch[u].rearrange("(c h) e s -> (h e) c s", c=DC), qT[:, u])\
                        .then_inc(q_saved[u], 16)
                for u in range(2):
                    sp.wait_ge(q_saved[u], 16 * (i + 1))
                    for a in range(A):
                        sp.dma_start(q_by_a[a * HD:a * HD + HD, u],
                                     q_scratch[u].rearrange("h e (a j) -> a e h j", a=A)[a]).then_inc(q_relaid[u], 16)
                for u in range(2):
                    sp.wait_ge(out_ready, 2 * i + u + 1)
                    to = o_scratch[u].rearrange("(a j) (h e) -> a h j e", a=A, h=HEADS)
                    for a in range(A):
                        sp.dma_start(to[a], out[a * HEADS:a * HEADS + HEADS, u]).then_inc(o_saved[u], 16)
                    sp.wait_ge(o_saved[u], 16 * A * (i + 1))
                    sp.dma_start(o[:, u], o_scratch[u].rearrange("(t p) d -> p t d", p=P)).then_inc(o_loaded[u], 16)
                if more:
                    for u in range(2):
                        sp.wait_ge(x_used, 2 * i + u + 1)
                        sp.dma_start(xin[:, u], batch_of(x_in, 2 * i + u + 2)).then_inc(x_loaded[u], 16)
                for u in range(2):
                    sp.wait_ge(y_ready, 2 * i + u + 1)
                    sp.dma_start(batch_of(x_out, 2 * i + u), yout[:, u]).then_inc(stored[u], 16)

            with sp.Fori(0, nb // 2 - 1) as i:
                turn_of_sp(i, True)
            turn_of_sp(nb // 2 - 1, False)
            for u in range(2):
                sp.wait_ge(stored[u], 16 * (nb // 2) + 16)

        @block.gpsimd
        def _(pool):
            pool.memset(half[:], -0.5)
            pool.wait_ge(loaded, 16 * len(loads))
            pool.tensor_scalar(bq_scaled[:], bq, SCALE, None, ALU.mult).then_inc(consts, 1)
            with pool.Fori(0, nb // 2) as i:
                for u in range(2):
                    pool.wait_ge(q_ready, 2 * i + u + 1)
                    for k in range(PARTS_Q):
                        cut = slice(k * PART_TILES, k * PART_TILES + PART_TILES)
                        wide = [P, PART_TILES, A, HEADS]
                        for c in range(DC):
                            pool.tensor_tensor(q_wide[:, u, c, cut].rearrange("p j (a h) -> p j a h", a=A),
                                               over(qT[:, u, c].rearrange("p (a j) -> p j a", a=A)[:, cut], HEADS),
                                               mask_h[:, c].unsqueeze(1).unsqueeze(1).broadcast_to(wide), ALU.mult)
                        if k == 0:
                            pool.wait_ge(q_relaid[u], 16 * A * (i + 1))
                        pool.tensor_tensor(q_dist[:, u, cut].rearrange("p j (a h) -> p j a h", a=A),
                                           q_by_a[:, u].rearrange("p h j -> p j h")[:, cut].unsqueeze(2)
                                           .broadcast_to(wide),
                                           over(mask_a[:], HEADS).unsqueeze(1).broadcast_to(wide),
                                           ALU.mult).then_inc(wide_ready, 1)
                for u in range(2):
                    pool.wait_ge(x_loaded[u], 16 * (i + 1))
                    pool.tensor_tensor(x_bo[:, u], xin[:, u], bo.unsqueeze(1).broadcast_to([P, TT, D]),
                                       ALU.add).then_inc(xbo_ready, 1)
                for u in range(2):
                    pool.wait_ge(var, 2 * i + u + 1)
                    pool.tensor_tensor(rs[:, u], ve[:, u], half[:], ALU.pow).then_inc(rstd, 1)

        @block.scalar
        def _(act):
            act.wait_ge(loaded, 16 * len(loads))
            act.wait_ge(consts, 1)
            with act.Fori(0, nb // 2) as i:
                for u in range(2):
                    act.wait_ge(turned, 2 * i + u + 1)
                    nc.scalar.activation(xT[:, u], tiles(bank[4 * u]), ACT.Copy).then_inc(xT_ready, 1)
                    for done, b, to, bias, scale, ready in ((q_mm, 1, qT, bq_scaled, SCALE, q_ready),
                                                            (k_mm, 2, kT, bk, 1.0, k_ready)):
                        act.wait_ge(done, 2 * i + u + 1)
                        for c in range(DC):
                            last = nc.scalar.activation(to[:, u, c, :], tiles(bank[4 * u + b])[:, c, :], ACT.Identity,
                                                        bias=bias[:, c:c + 1], scale=scale)
                        last.then_inc(ready, 1)
                for u in range(2):
                    n = 2 * i + u
                    for m in range(UNITS + 1):
                        if m < UNITS:
                            act.wait_ge(max_ready, n * UNITS + m + 1)
                            for e in range(2):
                                j = 2 * m + e
                                last = nc.scalar.activation(probs[:, m % 2, e], tiles(bank[m % 2])[:, e], ACT.Exp,
                                                            bias=nmx[:, j:j + 1], accum_out=sums[:, u, j:j + 1])
                            last.then_inc(probs_ready, 1)
                        if m >= 1:
                            k = m - 1
                            act.wait_ge(probs_turned, n * UNITS + k + 1)
                            if k >= 2 or u == 1:
                                act.wait_ge(values_mm, n * UNITS + k - 1)
                            nc.scalar.activation(pT[:, k % 2].rearrange("p e c k -> p (e c k)"), bank[2 + k % 2][:],
                                                 ACT.Copy).then_inc(pT_ready, 1)
                for u in range(2):
                    act.wait_ge(o_turned, 2 * i + u + 1)
                    nc.scalar.activation(oT[:, u], tiles(bank[4 * u]), ACT.Copy).then_inc(oT_ready, 1)

        @block.vector
        def _(dve):
            dve.wait_ge(loaded, 16 * len(loads))
            with dve.Fori(0, nb // 2) as i:
                for u in range(2):
                    dve.wait_ge(v_mm, 2 * i + u + 1)
                    dve.tensor_tensor(v[:, u], tiles(bank[4 * u + 3]), bv.unsqueeze(1).broadcast_to([P, TT, D]),
                                      ALU.add).then_inc(v_ready, 1)
                for u in range(2):
                    n = 2 * i + u
                    for m in range(UNITS + 2):
                        if m < UNITS:
                            at = slice(2 * m, 2 * m + 2)
                            dve.wait_ge(scores_mm, n * UNITS + m + 1)
                            dve.tensor_reduce(mx[:, at], tiles(bank[m % 2]), AX.X, ALU.max)
                            dve.drain()
                            dve.tensor_scalar(nmx[:, at], mx[:, at], -1.0, None, ALU.mult).then_inc(max_ready, 1)
                        if m >= 2:
                            k = m - 2
                            dve.drain()
                            dve.wait_ge(values_mm, n * UNITS + k + 1)
                            for e in range(2):
                                last = dve.tensor_tensor(kept[:, e],
                                                         bank[4 + k % 2 * 2 + e][:, 0:BLK * HD]
                                                         .rearrange("p (b d) -> p b d", d=HD),
                                                         over(own[:], HD), ALU.mult)
                            last.then_inc(kept_ready, 1)
                            dve.drain()
                            dve.tensor_reduce(out[:, u, 2 * k:2 * k + 2], kept[:].rearrange("p e b d -> p e d b"),
                                              AX.X, ALU.add)
                    dve.drain()
                    dve.reciprocal(rsum[:], sums[:, u])
                    dve.drain()
                    dve.tensor_tensor(out[:, u], out[:, u], over(rsum[:], HD), ALU.mult).then_inc(out_ready, 1)
                for u in range(2):
                    dve.wait_ge(o_mm, 2 * i + u + 1)
                    dve.wait_ge(xbo_ready, 2 * i + u + 1)
                    dve.wait_ge(stored[u], 16 * (i + 1))
                    dve.tensor_tensor(yout[:, u], tiles(bank[4 * u + 1]), x_bo[:, u], ALU.add).then_inc(x_used, 1)
                    dve.drain()
                    row_stats(dve, yout[:, u], st[:, u], mv[:, u], ve[:, u]).then_inc(var, 1)
                for u in range(2):
                    dve.wait_ge(rstd, 2 * i + u + 1)
                    normalise(dve, yout[:, u], yout[:, u], mv[:, u], rs[:, u])[-1].then_inc(y_ready, 1)

        @block.tensor
        def _(pe):
            pe.wait_ge(loaded, 16 * len(loads))
            with pe.Fori(0, nb // 2) as i:
                for u in range(2):
                    n = 2 * i + u
                    pe.wait_ge(x_loaded[u], 16 * (i + 1))
                    turn(pe, tiles(bank[4 * u]), xin[:, u], ident).then_inc(turned, 1)
                    pe.wait_ge(xT_ready, n + 1)
                    for b, wt, done in ((1, wq, q_mm), (2, wk, k_mm)):
                        for g in range(DC):
                            last = project(pe, tiles(bank[4 * u + b])[:, g], wt[:, :, g * P:g * P + P], xT[:, u])
                        last.then_inc(done, 1)
                    by_token(pe, tiles(bank[4 * u + 3]), xT[:, u], wv).then_inc(v_mm, 1)
                for u in range(2):
                    n = 2 * i + u
                    if u == 0:
                        pe.wait_ge(q_ready, n + 2)
                        pe.wait_ge(k_ready, n + 2)
                        pe.wait_ge(v_ready, n + 2)

                    def scores(m):
                        if m % (PART_TILES // 2) == 0:
                            pe.wait_ge(wide_ready, n * PARTS_Q + m // (PART_TILES // 2) + 1)
                        if m >= 2 or u == 1:
                            pe.wait_ge(probs_ready, n * UNITS + m - 1)
                        for e in range(2):
                            j = 2 * m + e
                            dst = tiles(bank[m % 2])[:, e]
                            for c in range(DC):
                                pe.matmul(dst, q_wide[:, u, c, j], kT[:, u, c], start=c == 0, stop=False)
                            last = pe.matmul(dst, q_dist[:, u, j], dist_k[:, TILES - 1 - j:TILES - 1 - j + SEQ],
                                             start=False, stop=True)
                        last.then_inc(scores_mm, 1)

                    def turn_probs(m):
                        pe.wait_ge(probs_ready, n * UNITS + m + 1)
                        if m >= 2 or u == 1:
                            pe.wait_ge(pT_ready, n * UNITS + m - 1)
                        for e in range(2):
                            for c in range(TT):
                                last = pe.transpose(bank[2 + m % 2][:, (2 * e + c) * P:(2 * e + c) * P + P],
                                                    probs[:, m % 2, e, c * P:c * P + P], ident[:])
                        last.then_inc(probs_turned, 1)

                    def values(m):
                        pe.wait_ge(pT_ready, n * UNITS + m + 1)
                        if m >= 2 or u == 1:
                            pe.wait_ge(kept_ready, n * UNITS + m - 1)
                        for e in range(2):
                            j, dst = 2 * m + e, bank[4 + m % 2 * 2 + e]
                            for c in range(TT):
                                pe.matmul(dst[:, 0:D], pT[:, m % 2, e, c], v[:, u, c], start=c == 0, stop=c == TT - 1)
                            for c in range(TT):
                                s = P * c + SEQ - 1 - TILES * (A - 1) - j
                                seen = dist_v[:, s:s + TILES * (A - 1) + 1:TILES]
                                last = pe.matmul(dst[:, D:D + P], pT[:, m % 2, e, c], seen,
                                                 start=c == 0, stop=c == TT - 1)
                        last.then_inc(values_mm, 1)

                    for m in range(UNITS + 2):
                        if m < UNITS:
                            scores(m)
                        if 1 <= m <= UNITS:
                            turn_probs(m - 1)
                        if m >= 2:
                            values(m - 2)
                for u in range(2):
                    if u == 1:
                        pe.wait_ge(kept_ready, (2 * i + 2) * UNITS)
                    pe.wait_ge(o_loaded[u], 16 * (i + 1))
                    turn(pe, tiles(bank[4 * u]), o[:, u], ident).then_inc(o_turned, 1)
                for u in range(2):
                    pe.wait_ge(oT_ready, 2 * i + u + 1)
                    by_token(pe, tiles(bank[4 * u + 1]), oT[:, u], wo).then_inc(o_mm, 1)


def mlstm_layer(nc, mem, bank, ident_in, x_in, x_out, w, nb):
    NH, DH = 4, 64

    def sb(name, shape, dt=F32, rows=P):
        return mem.enter_context(nc.sbuf_tensor("mls_" + name, [rows] + shape, dt))

    def sem(name):
        return nc.alloc_semaphore("mls_" + name)

    ident, mask, minus = sb("ident", [P]), sb("mask", [384]), sb("minus", [NH, P], rows=NH)
    w_gate, w_ctx = sb("w_gate", [3, DC, 2, NH]), sb("w_ctx", [DC, 2, NH])
    b_gate, out_w, scale = sb("b_gate", [2], rows=NH), sb("out_w", [D]), sb("scale", [D])
    half, ones = sb("half", [TT * NH]), sb("ones", [SEQ], rows=NH)
    xin, cin, cT, xT = sb("xin", [2, TT, D]), sb("cin", [2, TT, D]), sb("cT", [2, DC, SEQ]), sb("xT", [2, DC, SEQ])
    v = sb("v", [2, TT, NH, DH + 1])
    size, ex, ln1p, low = (sb(n, [2, SEQ], rows=NH) for n in ("size", "ex", "ln1p", "low"))
    logf, csum, a, m = sb("logf", [2, SEQ], rows=NH), sb("csum", [2, SEQ + 1], rows=NH), \
        sb("a", [2, SEQ], rows=NH), sb("m", [2, SEQ], rows=NH)
    top, floor_row = sb("top", [2, SEQ], rows=NH), sb("floor_row", [2, SEQ], rows=NH)
    percol = sb("percol", [2, 2, TT, NH])
    shifted, decay, c = sb("shifted", [2, 2, 384]), sb("decay", [2, 2, 384]), sb("c", [2, 2, 384])
    norm = sb("norm", [2, TT, 2])
    hn, sq = sb("hn", [2, TT, NH, DH]), sb("sq", [2, TT, NH, DH])
    s1, s2, s3 = sb("s1", [2, 8]), sb("s2", [2, 8]), sb("s3", [2, 8])
    y, yout = sb("y", [2, TT, D]), sb("yout", [2, TT, D])
    st, mv, ve, rs = sb("st", [2, TT, 6]), sb("mv", [2, TT, 2]), sb("ve", [2, 2]), sb("rs", [2, 2])

    loaded, consts = sem("loaded"), sem("consts")
    x_loaded, c_loaded = [sem(f"x_loaded{u}") for u in range(2)], [sem(f"c_loaded{u}") for u in range(2)]
    stored = [sem(f"stored{u}") for u in range(2)]
    turned, xT_ready, v_ready, ig_mm, fg_mm = (sem("turned"), sem("xT_ready"), sem("v_ready"), sem("ig_mm"),
                                               sem("fg_mm"))
    size_ready, ln_ready, m_ready, a_ready, top_ready, floor_ready = (
        sem("size_ready"), sem("ln_ready"), sem("m_ready"), sem("a_ready"), sem("top_ready"), sem("floor_ready"))
    percol_mm, percol_ready, m_mm, shifted_ready, decay_ready = (
        sem("percol_mm"), sem("percol_ready"), sem("m_mm"), sem("shifted_ready"), sem("decay_ready"))
    qk_mm, c_ready, h_mm, hn_part, cen_ready, sq_ready = (sem("qk_mm"), sem("c_ready"), sem("h_mm"),
                                                          sem("hn_part"), sem("cen_ready"), sem("sq_ready"))
    hvar, hrstd, hn_ready, out_ready, var, rstd, y_ready = (sem("hvar"), sem("hrstd"), sem("hn_ready"),
                                                            sem("out_ready"), sem("var"), sem("rstd"), sem("y_ready"))
    low_ready = sem("low_ready")

    loads = [(ident[:], ident_in), (mask[:], w["mask"]), (minus[:], w["minus"]), (w_gate[:], w["w_gate"]),
             (b_gate[:], w["b_gate"]), (out_w[:], w["out_w"].partition_broadcast(P))]

    def context(n):
        return w["contextT"][bass.ds(n, 1)].rearrange("a (c p) s -> p (a c) s", p=P)

    def flat(ap):
        return ap.rearrange("p t h e -> p (t h) e")

    with nc.Block() as block:
        @block.sync
        def _(sp):
            load_all(sp, loaded, loads)

            def load_context(n, u):
                sp.dma_start(cT[:, u], context(n)).then_inc(c_loaded[u], 16)
                sp.dma_start(cin[:, u], batch_of(w["context"], n)).then_inc(c_loaded[u], 16)
            stream_batches(sp, x_in, x_out, xin, yout, x_loaded, out_ready, y_ready, stored, nb, load_context)

        @block.gpsimd
        def _(pool):
            pool.memset(half[:], -0.5)
            pool.memset(ones[:], 1.0)
            pool.memset(csum[:], 0.0)
            pool.drain()
            pool.memset(v[:], 1.0)
            pool.wait_ge(loaded, 16 * len(loads))
            pool.tensor_tensor(w_ctx[:], w_gate[:, 1], w_gate[:, 2], ALU.add)
            pool.drain()
            pool.tensor_scalar(scale[:], out_w[:], 1.0, None, ALU.add).then_inc(consts, 1)
            with pool.Fori(0, nb // 2) as i:
                for u in range(2):
                    pool.wait_ge(hvar, 2 * i + u + 1)
                    pool.tensor_tensor(s3[:, u], s2[:, u], half[:], ALU.pow).then_inc(hrstd, 1)
                for u in range(2):
                    pool.wait_ge(hn_ready, 2 * i + u + 1)
                    pool.tensor_tensor(y[:, u], hn[:, u].rearrange("p t h e -> p t (h e)"),
                                       scale[:].unsqueeze(1).broadcast_to([P, TT, D]), ALU.mult)
                    pool.drain()
                    pool.tensor_tensor(y[:, u], y[:, u], xin[:, u], ALU.add).then_inc(out_ready, 1)
                for u in range(2):
                    pool.wait_ge(var, 2 * i + u + 1)
                    pool.tensor_tensor(rs[:, u], ve[:, u], half[:, 0:2], ALU.pow).then_inc(rstd, 1)

        @block.scalar
        def _(act):
            act.wait_ge(loaded, 16 * len(loads))
            act.wait_ge(consts, 1)
            with act.Fori(0, nb // 2) as i:
                for u in range(2):
                    act.wait_ge(turned, 2 * i + u + 1)
                    nc.scalar.activation(xT[:, u], tiles(bank[4 * u]), ACT.Copy).then_inc(xT_ready, 1)
                    act.wait_ge(c_loaded[u], 32 * (i + 1))
                    nc.scalar.activation(v[:, u, :, :, 0:DH], cin[:, u].rearrange("p t (h e) -> p t h e", e=DH),
                                         ACT.Copy).then_inc(v_ready, 1)
                for u in range(2):
                    n = 2 * i + u
                    act.wait_ge(fg_mm, n + 1)
                    nc.scalar.activation(size[:, u], bank[4 * u + 2][0:NH, 0:SEQ], ACT.Abs,
                                         bias=b_gate[:, 1:2]).then_inc(size_ready, 1)
                    act.drain()
                    nc.scalar.activation(ex[:, u], size[:, u], ACT.Exp, scale=-1.0)
                    act.drain()
                    nc.scalar.activation(ln1p[:, u], ex[:, u], ACT.Ln, bias=ones[:, 0:1]).then_inc(ln_ready, 1)
                for u in range(2):
                    act.wait_ge(top_ready, 2 * i + u + 1)
                    nc.scalar.activation(floor_row[:, u], top[:, u], ACT.Exp, scale=-1.0).then_inc(floor_ready, 1)
                for pair in range(2):
                    for u in range(2):
                        n = 2 * i + u
                        act.wait_ge(percol_ready, n + 1)
                        act.wait_ge(shifted_ready, 2 * (2 * i + pair) + u + 1)
                        for k in range(2):
                            for t, cut in enumerate((slice(0, 256), slice(256, 384))):
                                last = nc.scalar.activation(decay[:, u, k, cut], shifted[:, u, k, cut], ACT.Exp,
                                                            bias=percol[:, u, 0, t, 2 * pair + k:2 * pair + k + 1])
                        last.then_inc(decay_ready, 1)
                for u in range(2):
                    act.wait_ge(cen_ready, 2 * i + u + 1)
                    nc.scalar.activation(sq[:, u], hn[:, u], ACT.Square).then_inc(sq_ready, 1)

        @block.vector
        def _(dve):
            dve.wait_ge(loaded, 16 * len(loads))
            dve.wait_ge(consts, 1)
            with dve.Fori(0, nb // 2) as i:
                for u in range(2):
                    n = 2 * i + u
                    dve.wait_ge(size_ready, n + 1)
                    dve.tensor_scalar(low[:, u], bank[4 * u + 2][0:NH, 0:SEQ], b_gate[:, 1:2], 0.0,
                                      ALU.add, ALU.min).then_inc(low_ready, 1)
                    dve.wait_ge(low_ready, n + 1)
                    dve.wait_ge(ln_ready, n + 1)
                    dve.tensor_tensor(logf[:, u], low[:, u], ln1p[:, u], ALU.subtract)
                    dve.drain()
                    dve.tensor_tensor_scan(csum[:, u, 1:SEQ + 1], ones[:], logf[:, u], 0.0, ALU.mult, ALU.add)
                    dve.drain()
                    dve.wait_ge(ig_mm, n + 1)
                    dve.scalar_tensor_tensor(out=a[:, u], in0=bank[4 * u + 1][0:NH, 0:SEQ], scalar=b_gate[:, 0:1],
                                             in1=csum[:, u, 0:SEQ], op0=ALU.add, op1=ALU.subtract)\
                        .then_inc(a_ready, 1)
                    dve.drain()
                    dve.tensor_tensor_scan(m[:, u], a[:, u], a[:, u], -3.0e38, ALU.max, ALU.max)\
                        .then_inc(m_ready, 1)
                    dve.drain()
                    dve.tensor_tensor(top[:, u], csum[:, u, 1:SEQ + 1], m[:, u], ALU.add).then_inc(top_ready, 1)
                for u in range(2):
                    dve.wait_ge(percol_mm, 2 * i + u + 1)
                    dve.tensor_copy(percol[:, u].rearrange("p k t h -> p (k t h)"), bank[4 * u + 3][:, 0:16])\
                        .then_inc(percol_ready, 1)
                for pair in range(2):
                    for u in range(2):
                        p = 2 * (2 * i + pair) + u + 1
                        dve.wait_ge(m_mm, p)
                        b = tiles(bank[4 * u + 1])
                        dve.tensor_tensor(shifted[:, u, :, 0:256], b,
                                          mask[:, 0:256].unsqueeze(1).broadcast_to([P, 2, 256]), ALU.add)
                        dve.tensor_tensor(shifted[:, u, :, 256:384], b[:, :, P:256],
                                          mask[:, 256:384].unsqueeze(1).broadcast_to([P, 2, P]), ALU.add)\
                            .then_inc(shifted_ready, 1)
                    for u in range(2):
                        p = 2 * (2 * i + pair) + u + 1
                        dve.wait_ge(decay_ready, p)
                        dve.wait_ge(qk_mm, p)
                        for k in range(2):
                            last = dve.scalar_tensor_tensor(out=c[:, u, k], in0=bank[4 * u + 2 + k][:, 0:384],
                                                            scalar=DH ** -0.5, in1=decay[:, u, k],
                                                            op0=ALU.mult, op1=ALU.mult)
                        last.then_inc(c_ready, 1)
                    for u in range(2):
                        p = 2 * (2 * i + pair) + u + 1
                        dve.wait_ge(h_mm, p)
                        hp = bank[4 * u][:, 0:260].rearrange("p (t k e) -> p t k e", t=TT, k=2)
                        dve.scalar_tensor_tensor(out=norm[:, u], in0=hp[:, :, :, DH], scalar=-1.0,
                                                 in1=percol[:, u, 1, :, 2 * pair:2 * pair + 2],
                                                 op0=ALU.mult, op1=ALU.max)
                        dve.drain()
                        dve.tensor_tensor(norm[:, u], hp[:, :, :, DH], norm[:, u], ALU.max)
                        dve.drain()
                        dve.tensor_scalar(norm[:, u], norm[:, u], 1e-8, None, ALU.add)
                        dve.drain()
                        dve.reciprocal(norm[:, u], norm[:, u])
                        dve.drain()
                        dve.tensor_tensor(hn[:, u, :, 2 * pair:2 * pair + 2, :], hp[:, :, :, 0:DH],
                                          over(norm[:, u], DH), ALU.mult).then_inc(hn_part, 1)
                for u in range(2):
                    dve.tensor_reduce(s1[:, u], flat(hn[:, u]), AX.X, ALU.add)
                    dve.drain()
                    dve.tensor_scalar(s1[:, u], s1[:, u], 1.0 / DH, None, ALU.mult)
                    dve.drain()
                    dve.tensor_tensor(flat(hn[:, u]), flat(hn[:, u]), over(s1[:, u], DH), ALU.subtract)\
                        .then_inc(cen_ready, 1)
                for u in range(2):
                    dve.wait_ge(sq_ready, 2 * i + u + 1)
                    link(dve, dve.tensor_reduce(s2[:, u], flat(sq[:, u]), AX.X, ALU.add))
                    dve.tensor_scalar(s2[:, u], s2[:, u], 1.0 / DH, LN_EPS, ALU.mult, ALU.add).then_inc(hvar, 1)
                for u in range(2):
                    dve.wait_ge(hrstd, 2 * i + u + 1)
                    dve.tensor_tensor(flat(hn[:, u]), flat(hn[:, u]), over(s3[:, u], DH), ALU.mult)\
                        .then_inc(hn_ready, 1)
                for u in range(2):
                    dve.wait_ge(out_ready, 2 * i + u + 1)
                    row_stats(dve, y[:, u], st[:, u], mv[:, u], ve[:, u]).then_inc(var, 1)
                for u in range(2):
                    dve.wait_ge(rstd, 2 * i + u + 1)
                    dve.wait_ge(stored[u], 16 * (i + 1))
                    normalise(dve, yout[:, u], y[:, u], mv[:, u], rs[:, u])[-1].then_inc(y_ready, 1)

        @block.tensor
        def _(pe):
            pe.wait_ge(loaded, 16 * len(loads))
            pe.wait_ge(consts, 1)
            with pe.Fori(0, nb // 2) as i:
                for u in range(2):
                    pe.wait_ge(x_loaded[u], 16 * (i + 1))
                    turn(pe, tiles(bank[4 * u]), xin[:, u], ident).then_inc(turned, 1)
                for u in range(2):
                    n = 2 * i + u
                    pe.wait_ge(c_loaded[u], 32 * (i + 1))
                    pe.wait_ge(xT_ready, n + 1)
                    for b, kind, done in ((2, 1, fg_mm), (1, 0, ig_mm)):
                        out = bank[4 * u + b][0:NH, 0:SEQ]
                        for k in range(DC):
                            pe.matmul(out, w_gate[:, 0, k, kind], xT[:, u, k], start=k == 0, stop=False)
                        for k in range(DC):
                            last = pe.matmul(out, w_ctx[:, k, kind], cT[:, u, k], start=False, stop=k == DC - 1)
                        last.then_inc(done, 1)
                for u in range(2):
                    n = 2 * i + u
                    pe.wait_ge(a_ready, n + 1)
                    pe.wait_ge(floor_ready, n + 1)
                    for kind, row in ((0, a), (1, floor_row)):
                        for t in range(TT):
                            at = (kind * TT + t) * NH
                            out, row_t = bank[4 * u + 3][:, at:at + NH], row[:, u, t * P:t * P + P]
                            if kind == 0:
                                pe.matmul(out, row_t, ident[0:NH, 0:NH], start=True, stop=True)
                            else:
                                last = pe.transpose(out, row_t, ident[0:NH, 0:NH])
                    last.then_inc(percol_mm, 1)
                for pair in range(2):
                    for u in range(2):
                        n = 2 * i + u
                        p = 2 * (2 * i + pair) + u + 1
                        if pair == 0:
                            pe.wait_ge(m_ready, n + 1)
                            pe.wait_ge(percol_ready, n + 1)
                        for k in range(2):
                            last = pe.matmul(tiles(bank[4 * u + 1])[:, k, :], minus[:, 2 * pair + k, :], m[:, u],
                                             start=True, stop=True)
                        last.then_inc(m_mm, 1)
                        for k in range(2):
                            rows = slice(k * DH, k * DH + DH)
                            for t in range(TT):
                                last = pe.matmul(bank[4 * u + 2 + k][:, 256 * t:256 * t + 256 - P * t],
                                                 cT[rows, u, pair, t * P:t * P + P], xT[rows, u, pair, t * P:SEQ],
                                                 start=True, stop=True)
                        last.then_inc(qk_mm, 1)
                    for u in range(2):
                        n = 2 * i + u
                        pe.wait_ge(c_ready, 2 * (2 * i + pair) + u + 1)
                        pe.wait_ge(v_ready, n + 1)
                        if pair == 1:
                            pe.wait_ge(hn_part, 2 * (2 * i) + u + 1)
                        hp = bank[4 * u][:, 0:260].rearrange("p (t k e) -> p t k e", t=TT, k=2)
                        for k in range(2):
                            h = 2 * pair + k
                            pe.matmul(hp[:, 0, k, :], c[:, u, k, 0:P], v[:, u, 0, h], start=True, stop=True)
                            pe.matmul(hp[:, 1, k, :], c[:, u, k, P:256], v[:, u, 0, h], start=True, stop=False)
                            last = pe.matmul(hp[:, 1, k, :], c[:, u, k, 256:384], v[:, u, 1, h],
                                             start=False, stop=True)
                        last.then_inc(h_mm, 1)


def peer_layer(nc, mem, bank, ident_in, x_in, x_out, w, nb):
    PH, KD, NK, TOP = 8, 128, 64, 8
    BLOCKS = 2 * PH
    COLS = 32
    TOKENS = nb * SEQ
    CH = 32
    PICKS = PH * TOP

    def sb(name, shape, dt=F32, c=mem):
        return c.enter_context(nc.sbuf_tensor("per_" + name, [P] + shape, dt))

    def sem(name):
        return nc.alloc_semaphore("per_" + name)

    ident, ones, half = sb("ident", [P]), sb("ones", [P]), sb("half", [BLOCKS])
    down, up = sb("down", [DC, COLS, P]), sb("up", [COLS, D])
    w_sim, b_sim, neg_mean = sb("w_sim", [DC, BLOCKS * NK]), sb("b_sim", [BLOCKS * NK]), sb("neg_mean", [DC])
    loaded, consts, tables_loaded = sem("loaded"), sem("consts"), sem("tables_loaded")
    x_loaded = [sem(f"x_loaded{u}") for u in range(2)]

    with ExitStack() as pre:
        x = sb("x", [nb, TT, D], c=pre)
        xc = sb("xc", [nb, TT, D], c=pre)
        wq, wqT = sb("wq", [DC, BLOCKS, P], c=pre), sb("wqT", [BLOCKS, D], c=pre)
        keys, keys_scaled = sb("keys", [BLOCKS, NK], c=pre), sb("keys_scaled", [BLOCKS, NK], c=pre)
        gamma, beta = sb("gamma", [BLOCKS], c=pre), sb("beta", [BLOCKS], c=pre)
        beta_wide = sb("beta_wide", [BLOCKS, P], c=pre)
        mean, cov, prod = sb("mean", [D], c=pre), sb("cov", [DC, D], c=pre), sb("prod", [2, D], c=pre)
        qvar, qve, qrs, qscale = (sb(n, [BLOCKS], c=pre) for n in ("qvar", "qve", "qrs", "qscale"))
        sums_mm, mean_ready, xc_ready, cov_mm, cov_ready = (sem("sums_mm"), sem("mean_ready"), sem("xc_ready"),
                                                            sem("cov_mm"), sem("cov_ready"))
        mean_turned, col_ready, wcov_mm, var_taken, qve_ready = (sem("mean_turned"), sem("col_ready"),
                                                                 sem("wcov_mm"), sem("var_taken"), sem("qve_ready"))
        qrs_ready, keys_ready, beta_ready, bias_mm, bias_copied = (sem("qrs_ready"), sem("keys_ready"),
                                                                   sem("beta_ready"), sem("bias_mm"),
                                                                   sem("bias_copied"))
        wsim_mm, wsim_ready = sem("wsim_mm"), sem("wsim_ready")
        loads = [(ident[:], ident_in), (wq[:], w["wq"]), (wqT[:], w["wqT"]), (keys[:], w["keys"]),
                 (gamma[:], w["gamma"]), (beta[:], w["beta"])]
        per_bank = 512 // NK

        with nc.Block() as block:
            @block.sync
            def _(sp):
                for n in range(nb):
                    sp.dma_start(x[:, n], batch_of(x_in, n)).then_inc(x_loaded[0], 16)
                load_all(sp, loaded, loads)
                load_all(sp, tables_loaded, [(down[:], w["down"]), (up[:], w["up"])])
                sp.wait_ge(tables_loaded, 32)

            @block.gpsimd
            def _(pool):
                pool.memset(half[:], -0.5)
                pool.memset(ones[:], 1.0).then_inc(consts, 1)
                pool.drain()
                pool.wait_ge(qve_ready, 1)
                pool.tensor_tensor(qrs[:], qve[:], half[:], ALU.pow).then_inc(qrs_ready, 1)

            @block.scalar
            def _(act):
                act.wait_ge(cov_mm, 1)
                nc.scalar.activation(cov[:], tiles(bank[1]), ACT.Copy, scale=1.0 / TOKENS).then_inc(cov_ready, 1)
                act.wait_ge(mean_turned, 1)
                for c in range(DC):
                    last = nc.scalar.activation(neg_mean[:, c:c + 1], bank[2][:, c * P:c * P + 1], ACT.Copy,
                                                scale=-1.0)
                last.then_inc(col_ready, 1)
                act.wait_ge(bias_mm, 1)
                for k in range(2):
                    last = nc.scalar.activation(b_sim[:, k * 512:k * 512 + 512], bank[6 + k][:], ACT.Copy)
                last.then_inc(bias_copied, 1)
                for c in range(DC):
                    act.wait_ge(wsim_mm, c + 1)
                    for k in range(2):
                        last = nc.scalar.activation(w_sim[:, c, k * 512:k * 512 + 512], bank[2 * c + k][:], ACT.Copy)
                    last.then_inc(wsim_ready, 1)

            @block.vector
            def _(dve):
                dve.wait_ge(sums_mm, 1)
                dve.tensor_scalar(mean[:], bank[0][:, 0:D], 1.0 / TOKENS, None, ALU.mult).then_inc(mean_ready, 1)
                dve.drain()
                for n in range(nb):
                    dve.tensor_tensor(xc[:, n], x[:, n], mean[:].unsqueeze(1).broadcast_to([P, TT, D]),
                                      ALU.subtract).then_inc(xc_ready, 1)
                dve.wait_ge(loaded, 16 * len(loads))
                dve.tensor_copy(beta_wide[:], over(beta[:], P)).then_inc(beta_ready, 1)
                for b in range(BLOCKS):
                    dve.wait_ge(wcov_mm, b + 1)
                    dve.tensor_tensor(prod[:, b % 2], bank[3 + b % 3][:, 0:D], wqT[:, b], ALU.mult)\
                        .then_inc(var_taken, 1)
                    dve.drain()
                    dve.tensor_reduce(qvar[:, b:b + 1], prod[:, b % 2], AX.X, ALU.add)
                dve.drain()
                dve.tensor_scalar(qve[:], qvar[:], 1e-5, None, ALU.add).then_inc(qve_ready, 1)
                dve.wait_ge(qrs_ready, 1)
                dve.tensor_tensor(qscale[:], qrs[:], gamma[:], ALU.mult)
                dve.drain()
                dve.tensor_tensor(keys_scaled[:], keys[:], over(qscale[:], NK), ALU.mult).then_inc(keys_ready, 1)

            @block.tensor
            def _(pe):
                pe.wait_ge(consts, 1)
                pe.wait_ge(x_loaded[0], 16 * nb)
                for k in range(nb * TT):
                    last = pe.matmul(bank[0][:, 0:D], ones[:], x[:, k // TT, k % TT], start=k == 0,
                                     stop=k == nb * TT - 1)
                last.then_inc(sums_mm, 1)
                for c in range(DC):
                    for k in range(nb * TT):
                        pe.wait_ge(xc_ready, k // TT + 1)
                        last = pe.matmul(tiles(bank[1])[:, c], xc[:, k // TT, k % TT, c * P:c * P + P],
                                         xc[:, k // TT, k % TT], start=k == 0, stop=k == nb * TT - 1)
                last.then_inc(cov_mm, 1)
                pe.wait_ge(loaded, 16 * len(loads))
                for c in range(DC):
                    last = pe.transpose(bank[2][:, c * P:c * P + P], mean[:, c * P:c * P + P], ident[:])
                last.then_inc(mean_turned, 1)
                pe.wait_ge(cov_ready, 1)
                for b in range(BLOCKS):
                    if b >= 3:
                        pe.wait_ge(var_taken, b - 2)
                    for c in range(DC):
                        last = pe.matmul(bank[3 + b % 3][:, 0:D], wq[:, c, b], cov[:, c],
                                         start=c == 0, stop=c == DC - 1)
                    last.then_inc(wcov_mm, 1)
                pe.wait_ge(beta_ready, 1)
                for b in range(BLOCKS):
                    at = b % per_bank * NK
                    last = pe.matmul(bank[6 + b // per_bank][:, at:at + NK], beta_wide[:, b], keys[:, b],
                                     start=True, stop=True)
                last.then_inc(bias_mm, 1)
                pe.wait_ge(keys_ready, 1)
                pe.wait_ge(col_ready, 1)
                for c in range(DC):
                    for b in range(BLOCKS):
                        at = b % per_bank * NK
                        last = pe.matmul(bank[2 * c + b // per_bank][:, at:at + NK], wqT[:, b, c * P:c * P + P],
                                         keys_scaled[:, b], start=True, stop=True)
                    last.then_inc(wsim_mm, 1)

    iota_x, iota_y = sb("iota_x", [P], F16), sb("iota_y", [COLS], F16)
    iota_top = sb("iota_top", [TOP])
    xin = sb("xin", [2, TT, D])
    xT, xcT = sb("xT", [2, DC, SEQ]), sb("xcT", [2, DC, SEQ])
    act_w = sb("act_w", [2, COLS, SEQ])
    sim = sb("sim", [BLOCKS, NK])
    best, best_at = sb("best", [BLOCKS, TOP]), sb("best_at", [BLOCKS, TOP], U32)
    best_i = sb("best_i", [BLOCKS, TOP])
    pair = sb("pair", [PH, TOP * TOP])
    top, top_at = sb("top", [PH, TOP]), sb("top_at", [PH, TOP], U32)
    ranks_u, ranks = sb("ranks_u", [2, PICKS], U32), sb("ranks", [2, PICKS])
    hit = sim[:].rearrange("p b n -> p (b n)").rearrange("p (k m a) -> p k m a", k=2, a=TOP)
    ij, high = sb("ij", [2, PICKS]), sb("high", [PICKS])
    ex, esum = sb("ex", [PICKS]), sb("esum", [PH])
    picks = sb("picks", [2, TT, 3, 2, PICKS])
    weight_hi = sb("weight_hi", [PICKS], F16)
    picksT = sb("picksT", [2, 3, SEQ, 4], F16)
    NSLOT = 2
    hot_x, hot_y = sb("hot_x", [NSLOT, CH, P], F16), sb("hot_y", [NSLOT, CH, COLS], F16)
    yout = sb("yout", [2, TT, D])
    st, mv, ve, rs = sb("st", [2, TT, 6]), sb("mv", [2, TT, 2]), sb("ve", [2, 2]), sb("rs", [2, 2])

    x_read, x_used, iotas = [sem(f"x_read{u}") for u in range(2)], sem("x_used"), sem("iotas")
    stored = [sem(f"stored{u}") for u in range(2)]
    turned, xT_ready, sim_mm, sim_read = sem("turned"), sem("xT_ready"), sem("sim_mm"), sem("sim_read")
    hit_ready, hit_i_ready, ex_in, ex_ready, picks_ready = (sem("hit_ready"), sem("hit_i_ready"), sem("ex_in"),
                                                            sem("ex_ready"), sem("picks_ready"))
    picks_turned, picksT_ready, hot_ready, weights_mm, weighted = (
        sem("picks_turned"), sem("picksT_ready"), sem("hot_ready"), sem("weights_mm"), sem("weighted"))
    h_mm, gelu_ready, out_mm = sem("h_mm"), sem("gelu_ready"), sem("out_mm")
    var, rstd, y_ready = sem("var"), sem("rstd"), sem("y_ready")
    CHUNKS = SEQ // CH
    UNITS = SEQ // 16
    HU = COLS // 2
    SHARE = HU // TT
    OUT_BANK = (7, 0)

    with nc.Block() as block:
        @block.sync
        def _(sp):
            stream_batches(sp, x_in, x_out, xin, yout, x_read, x_used, y_ready, stored, nb)

        @block.gpsimd
        def _(pool):
            pool.iota(iota_x[:], [[1, P]], base=0, channel_multiplier=0, allow_small_or_imprecise_dtypes=True)
            pool.iota(iota_y[:], [[1, COLS]], base=0, channel_multiplier=0, allow_small_or_imprecise_dtypes=True)
            pool.iota(iota_top[:], [[1, TOP]], base=0, channel_multiplier=0, allow_small_or_imprecise_dtypes=True)\
                .then_inc(iotas, 1)
            pool.drain()
            with pool.Fori(0, nb // 2) as i:
                for u in range(2):
                    for t in range(TT):
                        pool.wait_ge(hit_ready, 2 * (2 * i + u) + t + 1)
                        for k in range(2):
                            idx = best_i[:, k * PH:k * PH + PH].unsqueeze(2).broadcast_to([P, PH, TOP, TOP])
                            o = hit[:, k].rearrange("p (h n) a -> p h n a", n=TOP)
                            last = pool.tensor_tensor(o, o, idx, ALU.mult)
                        last.then_inc(hit_i_ready, 1)
                for u in range(2):
                    pool.wait_ge(var, 2 * i + u + 1)
                    pool.tensor_tensor(rs[:, u], ve[:, u], half[:, 0:2], ALU.pow).then_inc(rstd, 1)

        @block.scalar
        def _(act):
            with act.Fori(0, nb // 2) as i:
                for u in range(2):
                    act.wait_ge(turned, 2 * i + u + 1)
                    for c in range(DC):
                        nc.scalar.activation(xcT[:, u, c, :], tiles(bank[2])[:, c], ACT.Identity,
                                             bias=neg_mean[:, c:c + 1])
                    nc.scalar.activation(xT[:, u], tiles(bank[2]), ACT.Copy).then_inc(xT_ready, 1)
                for u in range(2):
                    for k in range(HU):
                        m = (2 * i + u) * HU + k + 1
                        act.wait_ge(h_mm, m)
                        nc.scalar.activation(act_w[:, u, 2 * k:2 * k + 2, :], tiles(bank[3 + k % 2]),
                                             ACT.Gelu_apprx_tanh).then_inc(gelu_ready, 1)
                        if k % SHARE == SHARE - 2:
                            act.wait_ge(ex_in, TT * (2 * i + u) + k // SHARE + 1)
                            nc.scalar.activation(ex[:], ex[:], ACT.Exp).then_inc(ex_ready, 1)
                for u in range(2):
                    for t in range(TT):
                        act.wait_ge(picks_turned, 2 * (2 * i + u) + t + 1)
                        for k in range(3):
                            last = nc.scalar.activation(picksT[:, u, k, t * P:t * P + P, :],
                                                        over(bank[2][:, k * P:k * P + P], 4), ACT.Copy)
                        last.then_inc(picksT_ready, 1)

        @block.vector
        def _(dve):
            dve.wait_ge(iotas, 1)

            def select(i, u, t):
                m = 2 * (2 * i + u) + t + 1
                dve.wait_ge(sim_mm, m)
                for k in range(2):
                    last = dve.tensor_tensor(sim[:, k * PH:k * PH + PH].rearrange("p b n -> p (b n)"), bank[k][:],
                                             b_sim[:, k * 512:k * 512 + 512], ALU.add)
                last.then_inc(sim_read, 1)
                dve.drain()
                for b in range(BLOCKS):
                    dve.max(best[:, b], sim[:, b])
                dve.drain()
                for b in range(BLOCKS):
                    dve.max_index(best_at[:, b], best[:, b], sim[:, b])
                dve.tensor_tensor(pair[:].rearrange("p h (a b) -> p h a b", b=TOP), over(best[:, 0:PH], TOP),
                                  best[:, PH:BLOCKS].unsqueeze(2).broadcast_to([P, PH, TOP, TOP]), ALU.add)
                dve.drain()
                dve.tensor_copy(best_i[:], best_at[:])
                for h in range(PH):
                    dve.max(top[:, h], pair[:, h])
                dve.drain()
                for h in range(PH):
                    dve.max_index(top_at[:, h], top[:, h], pair[:, h])
                dve.drain()
                at = top_at[:].rearrange("p h n -> p (h n)")
                dve.tensor_scalar(ranks_u[:, 0], at, 3, None, ALU.logical_shift_right)
                dve.tensor_scalar(ranks_u[:, 1], at, 7, None, ALU.bitwise_and)
                dve.drain()
                dve.tensor_copy(ranks[:], ranks_u[:])
                dve.drain()
                for k in range(2):
                    last = dve.tensor_tensor(hit[:, k], over(ranks[:, k], TOP),
                                             iota_top[:].unsqueeze(1).broadcast_to([P, PICKS, TOP]), ALU.is_equal)
                last.then_inc(hit_ready, 1)
                dve.tensor_tensor(ex[:].rearrange("p (h n) -> p h n", n=TOP), top[:], over(top[:, :, 0], TOP),
                                  ALU.subtract).then_inc(ex_in, 1)
                dve.wait_ge(ex_ready, m)
                dve.tensor_reduce(esum[:], ex[:].rearrange("p (h n) -> p h n", n=TOP), AX.X, ALU.add)
                dve.drain()
                dve.reciprocal(esum[:], esum[:])
                dve.drain()
                dve.tensor_tensor(ex[:].rearrange("p (h n) -> p h n", n=TOP),
                                  ex[:].rearrange("p (h n) -> p h n", n=TOP), over(esum[:], TOP), ALU.mult)
                dve.drain()
                dve.tensor_copy(weight_hi[:], ex[:])
                dve.drain()
                s = picks[:, u, t]
                dve.tensor_copy(s[:, 2, 0], weight_hi[:])
                dve.tensor_tensor(s[:, 2, 1], ex[:], weight_hi[:], ALU.subtract)
                dve.wait_ge(hit_i_ready, m)
                dve.tensor_reduce(ij[:], hit, AX.X, ALU.add)
                dve.drain()
                dve.tensor_scalar(high[:], ij[:, 1], 32.0, None, ALU.is_ge)
                dve.drain()
                for k in range(2):
                    dve.scalar_tensor_tensor(out=s[:, 0, k], in0=high[:], scalar=64.0, in1=ij[:, 0],
                                             op0=ALU.mult, op1=ALU.add)
                    last = dve.scalar_tensor_tensor(out=s[:, 1, k], in0=high[:], scalar=-32.0, in1=ij[:, 1],
                                                    op0=ALU.mult, op1=ALU.add)
                last.then_inc(picks_ready, 1)

            def hot(i, u, k):
                slot, n = k % NSLOT, 2 * i + u
                cut = slice(k * CH, k * CH + CH)
                if k % 4 == 0:
                    dve.wait_ge(picksT_ready, TT * n + k // 4 + 1)
                wide_x, wide_y = [P, CH, P // 4, 4], [P, CH, COLS // 4, 4]

                def four(k, shape):
                    return picksT[:, u, k, cut, :].unsqueeze(2).broadcast_to(shape)

                def pattern(iota, shape):
                    return iota[:].rearrange("p (c e) -> p c e", e=4).unsqueeze(1).broadcast_to(shape)
                dve.tensor_tensor(hot_x[:, slot].rearrange("p s (c e) -> p s c e", e=4), four(0, wide_x),
                                  pattern(iota_x, wide_x), ALU.is_equal)
                hy = hot_y[:, slot].rearrange("p s (c e) -> p s c e", e=4)
                dve.tensor_tensor(hy, four(1, wide_y), pattern(iota_y, wide_y), ALU.is_equal)
                dve.drain()
                dve.tensor_tensor(hy, hy, four(2, wide_y), ALU.mult).then_inc(hot_ready, 1)

            def weigh(i, u, k):
                n = 2 * i + u
                dve.wait_ge(weights_mm, n * UNITS + k + 1)
                if k == 0:
                    dve.wait_ge(gelu_ready, (n + 1) * HU)
                g = act_w[:, u, :, k * 16:k * 16 + 16].rearrange("p j s -> p s j")
                dve.tensor_tensor(g, bank[5 + k % 2][:].rearrange("p (s j) -> p s j", j=COLS), g, ALU.mult)\
                    .then_inc(weighted, 1)

            with dve.Fori(0, nb // 2) as i:
                for u in range(2):
                    for t in range(TT):
                        select(i, u, t)
                for u in range(2):
                    hot(i, u, 0)
                    for k in range(CHUNKS):
                        if k + 1 < CHUNKS:
                            if k >= 1:
                                dve.wait_ge(weights_mm, (2 * i + u) * UNITS + 2 * k)
                            hot(i, u, k + 1)
                        weigh(i, u, 2 * k)
                        weigh(i, u, 2 * k + 1)
                for u in range(2):
                    dve.wait_ge(out_mm, 2 * i + u + 1)
                    dve.wait_ge(stored[u], 16 * (i + 1))
                    dve.tensor_tensor(yout[:, u], tiles(bank[OUT_BANK[u]]), xin[:, u], ALU.add).then_inc(x_used, 1)
                    dve.drain()
                    row_stats(dve, yout[:, u], st[:, u], mv[:, u], ve[:, u]).then_inc(var, 1)
                for u in range(2):
                    dve.wait_ge(rstd, 2 * i + u + 1)
                    normalise(dve, yout[:, u], yout[:, u], mv[:, u], rs[:, u])[-1].then_inc(y_ready, 1)

        @block.tensor
        def _(pe):
            with pe.Fori(0, nb // 2) as i:
                for u in range(2):
                    n = 2 * i + u
                    pe.wait_ge(x_read[u], 16 * (i + 1))
                    if u == 1:
                        pe.wait_ge(xT_ready, n)
                    turn(pe, tiles(bank[2]), xin[:, u], ident).then_inc(turned, 1)
                for step in range(2 * TT):
                    u, t = step // TT, step % TT
                    n = 2 * i + u
                    if t == 0:
                        pe.wait_ge(xT_ready, n + 1)
                    if step > 0:
                        pe.wait_ge(sim_read, TT * n + t)
                    for k in range(2):
                        for c in range(DC):
                            last = pe.matmul(bank[k][:], xcT[:, u, c, t * P:t * P + P],
                                             w_sim[:, c, k * 512:k * 512 + 512], start=c == 0, stop=c == DC - 1)
                    last.then_inc(sim_mm, 1)
                    for k in range(t * SHARE, t * SHARE + SHARE):
                        if k >= 2 or u == 1:
                            pe.wait_ge(gelu_ready, n * HU + k - 1)
                        for e in range(2):
                            last = project(pe, tiles(bank[3 + k % 2])[:, e], down[:, :, 2 * k + e, :], xT[:, u])
                        last.then_inc(h_mm, 1)
                for u in range(2):
                    n = 2 * i + u
                    for t in range(TT):
                        pe.wait_ge(picks_ready, TT * n + t + 1)
                        if u + t > 0:
                            pe.wait_ge(picksT_ready, TT * n + t)
                        for k in range(3):
                            last = pe.transpose(bank[2][:, k * P:k * P + P],
                                                picks[:, u, t, k].rearrange("p a n -> p (a n)"), ident[:])
                        last.then_inc(picks_turned, 1)

                def through_up(u, t, part):
                    if part == 0:
                        pe.wait_ge(weighted, (2 * i + u) * UNITS + (t + 1) * UNITS // TT)
                    for k in range(part * COLS // 8, (part + 1) * COLS // 8):
                        last = pe.matmul(tiles(bank[OUT_BANK[u]])[:, t, :], act_w[:, u, k, t * P:t * P + P],
                                         up[:, k, :], start=k == 0, stop=k == COLS - 1)
                    return last

                for u in range(2):
                    n = 2 * i + u
                    for k in range(UNITS):
                        if k % 2 == 0:
                            pe.wait_ge(hot_ready, n * CHUNKS + k // 2 + 1)
                        if k >= 2 or u == 1:
                            pe.wait_ge(weighted, n * UNITS + k - 1)
                        for s in range(16):
                            at = k % 2 * 16 + s
                            last = pe.matmul(bank[5 + k % 2][:, s * COLS:s * COLS + COLS],
                                             hot_x[:, k // 2 % NSLOT, at], hot_y[:, k // 2 % NSLOT, at],
                                             start=True, stop=True)
                        last.then_inc(weights_mm, 1)
                        if k >= UNITS // 2:
                            through_up(u, 0, k - UNITS // 2)
                        elif u == 1:
                            last = through_up(0, 1, k)
                            if k == UNITS // 2 - 1:
                                last.then_inc(out_mm, 1)
                for part in range(8):
                    last = through_up(1, 1, part)
                last.then_inc(out_mm, 1)


def chunks(a):
    return np.ascontiguousarray(a.reshape(DC, P, -1).transpose(1, 0, 2))


def padded_heads(a):
    lead = a.shape[:-1]
    out = np.zeros(lead + (HEADS, 32), a.dtype)
    out[..., :HD] = a.reshape(lead + (HEADS, HD))
    return out.reshape(lead + (HEADS * 32,))


def column(a, width=P):
    return np.ascontiguousarray(a.reshape(-1, P).T)


def padded(a, to):
    out = np.zeros(a.shape[:-1] + (to,), a.dtype)
    out[..., :a.shape[-1]] = a
    return out


def decay_table():
    gamma = 1.0 - np.exp2(-5.0 - np.arange(HEADS))
    key = np.arange(P)[:, None]
    out = np.zeros((P, HEADS, 384), np.float32)
    for cut, query in ((slice(0, 256), np.arange(256)[None]), (slice(256, 384), np.arange(128)[None])):
        diff = query - key
        for h in range(HEADS):
            out[:, h, cut] = np.where(diff >= 0, gamma[h] ** np.maximum(diff, 0), 0.0) * HD ** -0.5
    return out


def retention_arrays(a):
    def g(name):
        return np.asarray(a["L0_attn_" + name])
    b_in, w_in = g("b_in"), g("w_in")
    both = np.stack([padded(w_in[:, :HID], HC * P), padded(w_in[:, HID:], HC * P)], 1)
    return {
        "ret_cols": np.concatenate([column(g("norm1_w")), column(g("norm1_b")), column(g("norm2_w")),
                                    column(g("norm2_b")), column(g("bq")), column(g("bk")), column(padded(b_in[:HID], HC * P)),
                                    column(padded(b_in[HID:], HC * P))], 1),
        "ret_rows": np.stack([g("bv"), g("bg"), g("bo"), g("gn_w"), g("gn_b"), g("b_out")]),
        "ret_wq": chunks(g("wq")), "ret_wk": chunks(g("wk")),
        "ret_wv": chunks(g("wv")), "ret_wg": chunks(g("wg")), "ret_wo": chunks(g("wo")),
        "ret_decay": decay_table(),
        "ret_w_in": chunks(both.reshape(D, -1)).reshape(P, DC, 2, HC, P),
        "ret_w_out": np.ascontiguousarray(
            padded(g("w_out").T, HC * P).T.reshape(HC, P, D).transpose(1, 0, 2)),
    }


def cross_attention_arrays(a):
    def g(name):
        return np.asarray(a["L0_xattn_" + name])
    return {
        "xat_cols": np.concatenate([column(g("b_q")), column(g("b_k"))], 1),
        "xat_rows": np.stack([g("b_v"), g("b_o")]),
        "xat_wq": chunks(g("w_q").T), "xat_wk": chunks(g("w_k").T),
        "xat_wv": chunks(g("w_v").T), "xat_wo": chunks(g("w_o").T),
    }


def channel_mix_arrays(a):
    def g(name):
        return np.asarray(a["L0_ffn_" + name])
    return {
        "mix_mu": np.concatenate([column(g("mu_r")), column(g("mu_k"))], 1),
        "mix_wr": chunks(g("W_r").T), "mix_wk": chunks(g("W_k").T), "mix_wv": chunks(g("W_v").T),
    }


def mlstm_arrays(a):
    def g(name):
        return np.asarray(a["L1_xattn_" + name])
    heads = g("igate_w").shape[0]
    key, query = np.arange(P)[:, None], np.arange(P)[None]
    behind = np.where(key > query, np.float32(-1e30), np.float32(0))
    minus = np.zeros((heads, heads, P), np.float32)
    minus[np.arange(heads), np.arange(heads)] = -1.0
    gates = np.stack([g("igate_w"), g("fgate_w")])
    return {
        "mls_mask": np.concatenate([behind, np.zeros((P, P), np.float32), behind], 1),
        "mls_minus": minus,
        "mls_w_gate": np.ascontiguousarray(gates.reshape(2, heads, 3, DC, P).transpose(4, 2, 3, 0, 1)),
        "mls_b_gate": np.stack([g("igate_b"), g("fgate_b")], 1),
        "mls_out_w": g("out_w"),
    }


def peer_arrays(a):
    def g(name):
        return np.asarray(a["L1_ffn_" + name])
    blocks = g("w_q").shape[1] // P

    def by_code(table):
        return table.reshape(64, 2, 32, D).transpose(1, 0, 2, 3).reshape(P, 32, D)
    keys = g("keys")
    return {
        "per_wq": chunks(g("w_q")).reshape(P, DC, blocks, P),
        "per_wqT": np.ascontiguousarray(g("w_q").T.reshape(blocks, P, D).transpose(1, 0, 2)),
        "per_keys": np.ascontiguousarray(keys.transpose(3, 2, 0, 1).reshape(P, blocks, -1)),
        "per_gamma": column(g("bn_gamma")), "per_beta": column(g("bn_beta")),
        "per_down": np.ascontiguousarray(by_code(g("down_embed")).transpose(2, 1, 0)
                                         .reshape(DC, P, 32, P).transpose(1, 0, 2, 3)),
        "per_up": np.ascontiguousarray(by_code(g("up_embed"))),
    }


def relative_attention_arrays(a):
    def g(name):
        return np.asarray(a["L1_attn_" + name])
    w, b = g("W_qkv"), g("b_qkv")
    per = P // HEADS
    reach = 3 * P - (g("rel_emb_k").shape[0] // 2)

    def extended(table):
        return np.concatenate([np.repeat(table[:1], reach, 0), table, np.repeat(table[-1:], reach, 0)])
    row = np.arange(P)
    head_of_row = np.arange(DC)[None, :] * (P // HD) + row[:, None] // HD
    own_head = row[:, None] % HEADS == np.arange(HEADS)
    own_query = row[:, None] // HEADS == np.arange(per)[::-1]
    return {
        "rel_wq": chunks(w[:, :D]), "rel_wk": chunks(w[:, D:2 * D]), "rel_wv": chunks(w[:, 2 * D:]),
        "rel_wo": chunks(g("W_out")),
        "rel_cols": np.concatenate([column(b[:D]), column(b[D:2 * D])], 1),
        "rel_rows": np.stack([b[2 * D:], g("b_out")]),
        "rel_ext_kT": np.ascontiguousarray(extended(g("rel_emb_k")).T),
        "rel_ext_v": extended(g("rel_emb_v")),
        "rel_mask_h": (head_of_row[:, :, None] == np.arange(HEADS)).astype(np.float32),
        "rel_mask_a": (row[:, None] // HD == np.arange(per)).astype(np.float32),
        "rel_own": np.concatenate([own_head, own_query], 1).astype(np.float32),
    }


LAYERS = (("ret", retention_layer), ("xat", cross_attention_layer), ("mix", channel_mix_layer),
          ("rel", relative_attention_layer), ("mls", mlstm_layer), ("per", peer_layer))


def program(nc, at):
    with ExitStack() as banks:
        bank = [banks.enter_context(nc.psum_tensor(f"bank{k}", [P, 512], F32)) for k in range(8)]
        x_in = at["x"]
        for name, layer in LAYERS:
            last = name == LAYERS[-1][0]
            x_out = at["out"] if last else nc.dram_tensor("x_after_" + name, (BATCHES, SEQ, D), F32,
                                                          kind="Internal").ap()
            w = {k[4:]: v for k, v in at.items() if k.startswith(name + "_")}
            w.update(context=at["context"], contextT=at["contextT"])
            with nc.cleanup_on_exit(), ExitStack() as mem:
                layer(nc, mem, bank, at["ident"], x_in, x_out, w, BATCHES)
            x_in = x_out


def kernel(**inputs):
    import concourse.bacc as bacc
    from concourse.bass_utils import run_bass_kernel_spmd
    nc = bacc.Bacc("TRN2", target_bir_lowering=False, num_devices=1)
    context = np.asarray(inputs["ctx_1024"])
    arrays = {"x": np.asarray(inputs["x"]), "ident": np.eye(P, dtype=np.float32),
              "context": context, "contextT": np.ascontiguousarray(context.transpose(0, 2, 1))}
    for layout in (retention_arrays, cross_attention_arrays, channel_mix_arrays,
                   relative_attention_arrays, mlstm_arrays, peer_arrays):
        arrays.update(layout(inputs))
    at = {n: nc.dram_tensor("in_" + n, a.shape, mybir.dt.from_np(a.dtype), kind="ExternalInput").ap()
          for n, a in arrays.items()}
    at["out"] = nc.dram_tensor("out", (BATCHES, SEQ, D), F32, kind="ExternalOutput").ap()
    program(nc, at)
    r = run_bass_kernel_spmd(nc, [{"in_" + n: a for n, a in arrays.items()}], core_ids=[0])
    return r.results[0]["out"]
```
